# Optimizing a Trainium2 kernel written in Bass

```python
import numpy as np
import jax
import jax.numpy as jnp

def _softmax(x, axis=-1):
    return jax.nn.softmax(x, axis=axis)

def _gelu(x):
    return jax.nn.gelu(x, approximate=True)

def _silu(x):
    return jax.nn.silu(x)

def _sigmoid(x):
    return jax.nn.sigmoid(x)

def _layernorm(x, axis=-1, eps=1e-05):
    m = jnp.mean(x, axis=axis, keepdims=True)
    v = jnp.var(x, axis=axis, keepdims=True)
    return (x - m) / jnp.sqrt(v + eps)

def _scatter_add(tgt, idx, src, axis=0):
    return tgt.at[idx].add(src)

def _segment_sum(src, seg, n):
    return jax.ops.segment_sum(src, seg, n)
kernel_name = 'mk_gnn_resnorm_d2_gnn_r8_47d34a'

def setup_inputs(seed: int=0):
    np.random.seed(seed)
    _w = jnp.asarray

    def _rec_inputs():
        import jax
        import jax.numpy as jnp
        _gk = jax.random.key(seed)
        x = 0.0001712 + 1 * jax.random.normal(jax.random.fold_in(_gk, 1), (12500, 16), jnp.float32)
        _s = jax.random.randint(jax.random.fold_in(_gk, 2), (200000,), 0, 12500, jnp.int32)
        _d = jax.random.randint(jax.random.fold_in(_gk, 3), (200000,), 0, 12500, jnp.int32)
        _loop = jnp.arange(12500, dtype=jnp.int32)
        src = jnp.concatenate([_s, _d, _loop])
        dst = jnp.concatenate([_d, _s, _loop])
        _o = jnp.argsort(dst, stable=True)
        src = src[_o]
        dst = dst[_o]
        edge_attr_13 = 2.91757e-06 + 0.999892 * jax.random.normal(jax.random.fold_in(_gk, 12), (412500, 13), jnp.float32)
        return (x, src, dst, edge_attr_13)
    x, src, dst, edge_attr_13 = _rec_inputs()

    def _L0_gnn_setup():
        import jax, jax.numpy as jnp
        import numpy as np
        N = 6250
        E = 100000
        NC = 16
        FDIM = 13
        HID = 32
        NREPEATS = 2

        def _gru_cell(x, h, w_ih, w_hh, b_ih, b_hh):
            gi = x @ w_ih.T + b_ih
            gh = h @ w_hh.T + b_hh
            i_r, i_z, i_n = jnp.split(gi, 3, axis=1)
            h_r, h_z, h_n = jnp.split(gh, 3, axis=1)
            r = jax.nn.sigmoid(i_r + h_r)
            z = jax.nn.sigmoid(i_z + h_z)
            n = jnp.tanh(i_n + r * h_n)
            return (1.0 - z) * n + z * h
        key = jax.random.key(seed)
        ks = jax.random.split(key, 10)
        hx = jax.random.normal(ks[0], (N, NC), dtype=jnp.float32)
        edgefeats = jax.random.normal(ks[1], (E, FDIM), dtype=jnp.float32)
        edge_src = jax.random.randint(ks[2], (E,), 0, N, dtype=jnp.int32)
        edge_dst = jax.random.randint(ks[3], (E,), 0, N, dtype=jnp.int32)
        fnet_w1 = jax.random.normal(ks[4], (FDIM, HID), dtype=jnp.float32) * (1.0 / np.sqrt(FDIM))
        fnet_b1 = jnp.zeros((HID,), dtype=jnp.float32)
        fnet_w2 = jax.random.normal(ks[5], (HID, NC * NC), dtype=jnp.float32) * (0.1 / np.sqrt(HID))
        fnet_b2 = jnp.zeros((NC * NC,), dtype=jnp.float32)
        gru_w_ih = jax.random.normal(ks[6], (3 * NC, NC), dtype=jnp.float32) * (1.0 / np.sqrt(NC))
        gru_w_hh = jax.random.normal(ks[7], (3 * NC, NC), dtype=jnp.float32) * (1.0 / np.sqrt(NC))
        gru_b_ih = jnp.zeros((3 * NC,), dtype=jnp.float32)
        gru_b_hh = jnp.zeros((3 * NC,), dtype=jnp.float32)
        return {'hx': hx, 'edgefeats': edgefeats, 'edge_src': edge_src, 'edge_dst': edge_dst, 'fnet_w1': fnet_w1, 'fnet_b1': fnet_b1, 'fnet_w2': fnet_w2, 'fnet_b2': fnet_b2, 'gru_w_ih': gru_w_ih, 'gru_w_hh': gru_w_hh, 'gru_b_ih': gru_b_ih, 'gru_b_hh': gru_b_hh}
    _L0_gnn_all = _L0_gnn_setup()
    _L0_gnn_in = {k: v for k, v in _L0_gnn_all.items() if k in ('fnet_w1', 'fnet_b1', 'fnet_w2', 'fnet_b2', 'gru_w_ih', 'gru_w_hh', 'gru_b_ih', 'gru_b_hh')}
    del _L0_gnn_all

    def _L1_gnn_setup():
        import jax, jax.numpy as jnp
        import numpy as np
        N_NODES = 12500
        N_EDGES = 400000
        D_FEAT = 16
        key = jax.random.key(seed)
        kx, ke = jax.random.split(key)
        x = jax.random.normal(kx, (N_NODES, D_FEAT), dtype=jnp.float32)
        edge_index = jax.random.randint(ke, (2, N_EDGES), 0, N_NODES, dtype=jnp.int64)
        return {'x': x, 'edge_index': edge_index}
    _L1_gnn_all = _L1_gnn_setup()
    _L1_gnn_in = {k: v for k, v in _L1_gnn_all.items() if k in ()}
    del _L1_gnn_all
    return {'x': x, 'src': src, 'dst': dst, 'edge_attr_13': edge_attr_13, 'L0_gnn_fnet_w1': _L0_gnn_in['fnet_w1'], 'L0_gnn_fnet_b1': _L0_gnn_in['fnet_b1'], 'L0_gnn_fnet_w2': _L0_gnn_in['fnet_w2'], 'L0_gnn_fnet_b2': _L0_gnn_in['fnet_b2'], 'L0_gnn_gru_w_ih': _L0_gnn_in['gru_w_ih'], 'L0_gnn_gru_w_hh': _L0_gnn_in['gru_w_hh'], 'L0_gnn_gru_b_ih': _L0_gnn_in['gru_b_ih'], 'L0_gnn_gru_b_hh': _L0_gnn_in['gru_b_hh']}

def reference(x, src, dst, edge_attr_13, L0_gnn_fnet_w1, L0_gnn_fnet_b1, L0_gnn_fnet_w2, L0_gnn_fnet_b2, L0_gnn_gru_w_ih, L0_gnn_gru_w_hh, L0_gnn_gru_b_ih, L0_gnn_gru_b_hh):
    import jax
    import jax.numpy as jnp

    def _L0_gnn_ref(hx, edgefeats, edge_src, edge_dst, fnet_w1, fnet_b1, fnet_w2, fnet_b2, gru_w_ih, gru_w_hh, gru_b_ih, gru_b_hh):
        import jax, jax.numpy as jnp
        import numpy as np
        N = 6250
        E = 100000
        NC = 16
        FDIM = 13
        HID = 32
        NREPEATS = 2

        def _gru_cell(x, h, w_ih, w_hh, b_ih, b_hh):
            gi = x @ w_ih.T + b_ih
            gh = h @ w_hh.T + b_hh
            i_r, i_z, i_n = jnp.split(gi, 3, axis=1)
            h_r, h_z, h_n = jnp.split(gh, 3, axis=1)
            r = jax.nn.sigmoid(i_r + h_r)
            z = jax.nn.sigmoid(i_z + h_z)
            n = jnp.tanh(i_n + r * h_n)
            return (1.0 - z) * n + z * h
        n_nodes, nc = hx.shape
        w = jax.nn.relu(edgefeats @ fnet_w1 + fnet_b1) @ fnet_w2 + fnet_b2
        W = w.reshape(-1, nc, nc)
        deg = jax.ops.segment_sum(jnp.ones((edge_dst.shape[0],), hx.dtype), edge_dst, num_segments=n_nodes)
        inv_deg = 1.0 / jnp.maximum(deg, 1.0)
        for _ in range(NREPEATS):
            xj = hx[edge_src]
            m = jnp.einsum('ei,eio->eo', xj, W)
            agg = jax.ops.segment_sum(m, edge_dst, num_segments=n_nodes)
            agg = agg * inv_deg[:, None]
            hx = _gru_cell(agg, hx, gru_w_ih, gru_w_hh, gru_b_ih, gru_b_hh)
        return hx

    def _L1_gnn_ref(x, edge_index):
        import jax, jax.numpy as jnp
        import numpy as np
        N_NODES = 12500
        N_EDGES = 400000
        D_FEAT = 16
        row = edge_index[0]
        col = edge_index[1]
        msg = jnp.take(x, col, axis=0)
        tmp = jnp.take(msg, col, axis=0)
        out = jax.ops.segment_sum(tmp, row, num_segments=x.shape[0])
        return out
    edge_index = jnp.stack([src, dst])
    x = _layernorm(x + _L0_gnn_ref(x, edge_attr_13, src, dst, L0_gnn_fnet_w1, L0_gnn_fnet_b1, L0_gnn_fnet_w2, L0_gnn_fnet_b2, L0_gnn_gru_w_ih, L0_gnn_gru_w_hh, L0_gnn_gru_b_ih, L0_gnn_gru_b_hh), axis=-1)
    x = _layernorm(x + _L1_gnn_ref(x, edge_index), axis=-1)
    return x

_drawn_inputs = setup_inputs


def setup_inputs(seed=0):
    import zlib

    import numpy as np

    out = dict(_drawn_inputs(seed))
    spreads = {'L0_gnn_fnet_b1': (0.0, 2.0),
     'L0_gnn_fnet_b2': (0.0, 0.1),
     'L0_gnn_gru_b_ih': (0.0, 0.1),
     'L0_gnn_gru_b_hh': (0.0, 0.1)}
    factors = {'edge_attr_13': 3.704, 'L0_gnn_fnet_w1': 3.881}
    for name, (base, spread) in spreads.items():
        noise = np.random.default_rng([zlib.crc32(name.encode()), seed]).standard_normal(out[name].shape)
        drawn = base * np.exp(spread * noise) if base else spread * noise
        out[name] = jnp.asarray(drawn.astype(out[name].dtype))
    for name, factor in factors.items():
        out[name] = (out[name] * factor).astype(out[name].dtype)
    return out
```

```python
from contextlib import ExitStack

import concourse.bass as bass
from concourse import mybir
from concourse.alu_op_type import AluOpType as ALU

F32 = mybir.dt.float32
I32 = mybir.dt.int32
ACT = mybir.ActivationFunctionType
AX = mybir.AxisListType.X

P = 128
NODES, NC = 12500, 16
EDGES, FD = 412500, 13
HID = 32
REPEATS = 2
OT = 8
G = 24
OC = G // OT
CE = P * G
FULL = EDGES // CE
CHUNKS = FULL + 1
TE = P * OT
PAIRS = FULL // 2
SIX = 2 * OC
OCTETS = FULL * OC + 1
DUP = TE - (EDGES - FULL * CE)
assert FULL % 2 == 0 and 0 <= DUP and G % OT == 0
NP_, NJ = 125, 100
ROWS = 99 * P
MW = NC * NC
AW = MW + NC + 1
GW = 2 * NC + 1
GT = 4
GU = NJ // GT
ACCS = 8
EPS = 1e-5
TILES = EDGES // P
TDUP = P - EDGES % P
assert EDGES % P and TDUP > 0

PROD0, XC0, HALF0, W0, EDGE0 = 4 * SIX, SIX, 2, 8, SIX
ADDS = 16 * (2 + CHUNKS)


def program(nc, x, src, dst, ef, w1, b1, w2, b2, wih, whh, bih, bhh, out):
    with ExitStack() as ctx:
        def sb(name, shape, dt=F32):
            return ctx.enter_context(nc.sbuf_tensor(name, shape, dt))

        def sem(name):
            return ctx.enter_context(nc.semaphore(name))

        def hold(eng, s, value):
            eng.wait_ge(s, value)
            eng.nop(nofuse=True)

        hx_tab = nc.dram_tensor("hx_tab", [NODES, NC], F32).ap()
        agg = nc.dram_tensor("agg", [ROWS, GW], F32).ap()
        x2_tab = nc.dram_tensor("x2_tab", [NODES, NC], F32).ap()
        y_tab = nc.dram_tensor("y_tab", [ROWS, NC], F32).ap()
        acc = [nc.dram_tensor(f"acc{k}", [ROWS, NC], F32).ap() for k in range(ACCS)]

        ident = sb("ident", [P, P])
        before = sb("before", [P, P])
        cols = sb("col_no", [P, P])
        part = sb("part_no", [P, 1])
        dummy = sb("spare", [P, 1])
        zeros = sb("zeros", [P, ROWS * GW // P])
        w1bd = sb("w1bd", [4 * FD, 4 * HID])
        b1c = sb("b1c", [P, 1])
        w2s = sb("w2s", [P, MW])
        wc = sb("wc", [3 * NC + 2, 4 * NC])
        b2t = sb("b2t", [NC, NC])
        wiht = sb("wiht", [NC, 3 * NC])

        dst_i = sb("dst_i", [P, OCTETS * OT], I32)
        dst_rel = sb("dst_rel", [P, OCTETS * OT])
        span = sb("span", [P, 2, CHUNKS])
        spanr = sb("spanr", [P, 2, CHUNKS])
        width = sb("width", [P, CHUNKS])
        base_f = sb("base_f", [P, CHUNKS])
        base_i = sb("base_i", [P, CHUNKS], I32)
        rows_i = sb("rows_i", [P, CHUNKS], I32)
        widest = sb("widest", [P, 1])
        windowed = sb("windowed", [P, 1], I32)

        src_i = sb("src_i", [P, 2, G], I32)
        ef_sb = sb("ef_sb", [P, 2, G * FD])
        eft = sb("eft", [4 * FD, 2, 2 * P])
        ht = sb("ht", [P, 2, 2 * P])
        xg = sb("xg", [P, SIX, OT, NC])
        onehot = sb("onehot", [P, 2, OT, P])
        prod = sb("prod", [P, 2, OT, AW])
        win = sb("win", [P, 2, GW])
        win_rows = sb("win_rows", [P, 2], I32)

        xs = sb("xs", [NP_, NJ, NC])
        aggl = sb("aggl", [NP_, NJ, GW])
        gin = sb("gin", [NP_, NJ, 3 * NC + 2])
        gin_four = sb("gin_four", [NP_, 2, GT, 3 * NC + 2])
        gint = sb("gint", [3 * NC + 2, 2, GT * NP_])
        gates = sb("gates", [NP_, NJ, 4 * NC])
        inv = sb("inv", [NP_, NJ])
        stat = sb("stat", [NP_, 3, NJ])

        yidx = sb("yidx", [NP_, 2, 10], I32)
        yg = sb("yg", [NP_, 2, 10, NC])
        ywin = sb("ywin", [P, 2, NC])
        srcf = sb("srcf", [P, 2, OT])
        oht = sb("oht", [P, 2, OT * P])
        same = sb("same", [P, 2, OT, P])
        earlier = sb("earlier", [P, OT, P])
        count = sb("count", [P, OT])
        away = sb("away", [P, OT])
        shift = sb("shift", [P, OT])
        vals = sb("vals", [P, 2, OT, NC])
        merged = sb("merged", [P, 3, OT, NC])
        rows = sb("rows", [P, 3, OT], I32)

        bank = [ctx.enter_context(nc.psum_tensor(f"bank{k}", [P, 512], F32)) for k in range(8)]

        g_src = sb("g_src", [P, 1], I32)
        g_dst = sb("g_dst", [P, 1], I32)
        g_ef = sb("g_ef", [P, FD])
        g_x = sb("g_x", [P, NC])
        g_prod = sb("g_prod", [P, MW])
        g_vals = sb("g_vals", [P, GW])
        g_key = sb("g_key", [P, 1])
        g_valid = sb("g_valid", [P, 1])
        g_same = sb("g_same", [P, P])
        g_early = sb("g_early", [P, P])
        g_count = sb("g_count", [P, 1])
        g_away = sb("g_away", [P, 1])
        g_rows = sb("g_rows", [P, 1], I32)
        g_sum = sb("g_sum", [P, GW])

        consts = sem("consts")
        weights = sem("weights")
        w1_zero = sem("w1_zero")
        wc_zero = sem("wc_zero")
        dst_in = sem("dst_in")
        prep = sem("prep")
        spans_out = sem("spans_out")
        masked = sem("masked")
        b2w = sem("b2w")
        table = sem("table")
        src_in = [sem(f"src_in{k}") for k in range(2)]
        ef_in = [sem(f"ef_in{k}") for k in range(2)]
        ef_turned = sem("ef_turned")
        ef_copied = sem("ef_copied")
        h_summed = sem("h_summed")
        h_done = sem("h_done")
        w_done = sem("w_done")
        gathered = [sem(f"gathered{k}") for k in range(SIX)]
        prod_done = sem("prod_done")
        x_copied = sem("x_copied")
        hot_done = sem("hot_done")
        octet_summed = sem("octet_summed")
        win_out = sem("win_out")
        agg_rows = sem("agg_rows")
        agg_in = sem("agg_in")
        gin_done = sem("gin_done")
        gin_staged = sem("gin_staged")
        gin_turned = sem("gin_turned")
        gin_copied = sem("gin_copied")
        gate_summed = sem("gate_summed")
        gate_copied = sem("gate_copied")
        act_gates = sem("act_gates")
        own = sem("own")
        own1 = sem("own1")
        x2_out = sem("x2_out")
        ln_sqrt = sem("ln_sqrt")
        y_zero = sem("y_zero")
        yidx_in = [sem(f"yidx_in{k}") for k in range(2)]
        y_in = [sem(f"y_in{k}") for k in range(2)]
        y_out = [sem(f"y_out{k}") for k in range(2)]
        ywin_in = [sem(f"ywin_in{k}") for k in range(2)]
        s1_in = [sem(f"s1_in{k}") for k in range(2)]
        hot1 = sem("hot1")
        turned1 = sem("turned1")
        oht_done = sem("oht_done")
        same_done = sem("same_done")
        rows_done = sem("rows_done")
        v_done = sem("v_done")
        v_copied = sem("v_copied")
        m_done = sem("m_done")
        m_copied = sem("m_copied")
        acc_rows = [sem(f"acc_rows{k}") for k in range(ACCS)]
        scattered = sem("scattered")
        acc_in = sem("acc_in")
        acc_used = sem("acc_used")
        result = sem("result")
        out_done = sem("out_done")

        sums_done = sem("sums_done")
        acc_done = sem("acc_done")
        baton = sem("baton")
        g_in = sem("g_in")
        g_gathered = sem("g_gathered")
        g_own = sem("g_own")

        block = ctx.enter_context(nc.Block())

        def fits(eng):
            eng.wait_ge(prep, PREP_FLAG)
            return eng.value_load(windowed[0:1, 0:1], min_val=0, max_val=1)

        def tiles(eng, tile):
            with eng.Fori(0, TILES) as t:
                tile(t, False)
            tile(TILES, True)

        NSLOT = [PAIRS + 1] + [PAIRS] * (SIX - 1)
        NCH = [PAIRS + 1, PAIRS]
        SRC_FULL = src[0:FULL * CE].rearrange("(c p g) -> c p g", p=P, g=G)
        EF_FULL = ef[0:FULL * CE, :].rearrange("(c p g) f -> c p (g f)", p=P, g=G)
        SRC_TAIL = src[EDGES - TE:EDGES].rearrange("(p g) -> p g", g=OT)
        EF_TAIL = ef[EDGES - TE:EDGES, :].rearrange("(p g) f -> p (g f)", g=OT)

        @block.sync
        def _(sp):
            def src_load(c, par, ring_in):
                if c is None:
                    sp.dma_start(src_i[:, par, 0:OT], SRC_TAIL).then_inc(ring_in[par], 16)
                else:
                    sp.dma_start(src_i[:, par, :], SRC_FULL[bass.ds(c, 1), :, :].rearrange("a p g -> (a p) g")
                                 ).then_inc(ring_in[par], 16)

            sp.dma_start(dst_i[:, 0:FULL * G].rearrange("p (c g) -> p c g", g=G),
                         dst[0:FULL * CE].rearrange("(c p g) -> p c g", p=P, g=G)).then_inc(dst_in, 16)
            sp.dma_start(dst_i[:, FULL * G:], dst[EDGES - TE:EDGES].rearrange("(p g) -> p g", g=OT)
                         ).then_inc(dst_in, 16)
            sp.dma_start(hx_tab, x).then_inc(table, 16)
            sp.dma_start(xs[:, :, :], x.rearrange("(p j) f -> p j f", j=NJ)).then_inc(dst_in, 16)
            sp.wait_ge(w1_zero, 1)
            for k in range(4):
                sp.dma_start(w1bd[FD * k:FD * (k + 1), HID * k:HID * (k + 1)], w1).then_inc(weights, 16)
                sp.dma_start(b1c[HID * k:HID * (k + 1), :], b1.rearrange("(k a) -> k a", a=1)).then_inc(weights, 16)
                sp.dma_start(w2s[HID * k:HID * (k + 1), :], w2).then_inc(weights, 16)
            sp.wait_ge(wc_zero, 1)
            with nc.allow_non_contiguous_dma(reason="768 weights, once"):
                sp.dma_start(wiht[:, :], wih.rearrange("o i -> i o")).then_inc(weights, 16)
                sp.dma_start(b2t[:, :], b2.rearrange("(i o) -> o i", o=NC)).then_inc(weights, 16)
                sp.dma_start(wc[NC:2 * NC, 0:3 * NC], wih.rearrange("o i -> i o")).then_inc(weights, 16)
                sp.dma_start(wc[2 * NC:3 * NC, 0:2 * NC], whh[0:2 * NC, :].rearrange("o i -> i o")
                             ).then_inc(weights, 16)
                sp.dma_start(wc[2 * NC:3 * NC, 3 * NC:4 * NC], whh[2 * NC:3 * NC, :].rearrange("o i -> i o")
                             ).then_inc(weights, 16)
            brow = lambda v: v.rearrange("(a k) -> a k", a=1)
            sp.dma_start(wc[3 * NC:3 * NC + 1, 0:3 * NC], brow(bih)).then_inc(weights, 16)
            sp.dma_start(wc[3 * NC + 1:3 * NC + 2, 0:2 * NC], brow(bhh[0:2 * NC])).then_inc(weights, 16)
            sp.dma_start(wc[3 * NC + 1:3 * NC + 2, 3 * NC:4 * NC], brow(bhh[2 * NC:3 * NC])).then_inc(weights, 16)
            sp.wait_ge(consts, 1)

            sp.dma_start(y_tab[NODES:ROWS, :].rearrange("(p r) f -> p (r f)", p=86), zeros[0:86, 0:2 * NC]
                         ).then_inc(y_zero, 16)

            flag = fits(sp)

            def g_load(first_step, t, last, attributes):
                hold(sp, baton, first_step + 1)
                e = EDGES - P if last else t * P
                sp.dma_start(g_src[:, :], src[bass.ds(e, P)].rearrange("(p a) -> p a", a=1)).then_inc(g_in, 16)
                sp.dma_start(g_dst[:, :], dst[bass.ds(e, P)].rearrange("(p a) -> p a", a=1)).then_inc(g_in, 16)
                if attributes:
                    sp.dma_start(g_ef[:, :], ef[bass.ds(e, P), :]).then_inc(g_in, 16)

            with sp.Fori(0, REPEATS) as r:
                def load0(c, par, ck):
                    sp.wait_ge(ef_turned, EDGE0 + r * OCTETS + (ck - 1) * OC)
                    if c is None:
                        sp.dma_start(ef_sb[:, par, 0:OT * FD], EF_TAIL).then_inc(ef_in[par], 16)
                    else:
                        sp.dma_start(ef_sb[:, par, :], EF_FULL[bass.ds(c, 1), :, :].rearrange("a p g -> (a p) g")
                                     ).then_inc(ef_in[par], 16)
                    sp.wait_ge(prod_done, PROD0 + (r * OCTETS + (ck - 1) * OC) * 4)
                    src_load(c, par, src_in)

                with sp.If(flag > 0):
                    with sp.Fori(0, PAIRS) as i:
                        for par in range(2):
                            load0(i * 2 + par, par, i * 2 + par)
                    load0(None, 0, FULL)
                with sp.Else():
                    tiles(sp, lambda t, last: g_load((r * (TILES + 1) + t) * STEPS0, t, last, True))
                sp.wait_ge(sums_done, r + 1)
                sp.dma_start(aggl[:, :, :], agg[0:NODES, :].rearrange("(p j) f -> p j f", j=NJ)).then_inc(agg_in, 16)
                sp.wait_ge(own, own_base(r + 1))
                sp.dma_start(hx_tab.rearrange("(p j) f -> p j f", j=NJ), gin[:, :, 2 * NC:3 * NC]).then_inc(table, 16)
            sp.wait_ge(own, OWN_X2)
            sp.dma_start(x2_tab.rearrange("(p j) f -> p j f", j=NJ), xs[:, :, :]).then_inc(x2_out, 16)

            YI = dst[0:NODES].rearrange("(p b k) -> b p k", p=NP_, k=10)
            YO = y_tab[0:NODES, :].rearrange("(p b k) f -> b p (k f)", p=NP_, k=10)
            for par in range(2):
                sp.dma_start(yidx[:, par, :], YI[par]).then_inc(yidx_in[par], 16)
            def y_store(i, last=False):
                for par in range(2):
                    sp.wait_ge(y_in[par], 160 * (i + 1))
                    sp.dma_start(YO[bass.ds(i * 2 + par, 1), :, :].rearrange("a p k -> (a p) k"),
                                 yg[:, par, :, :].rearrange("p k f -> p (k f)")).then_inc(y_out[par], 16)
                    if not last:
                        sp.dma_start(yidx[:, par, :], YI[bass.ds(i * 2 + par + 2, 1), :, :].rearrange(
                            "a p k -> (a p) k")).then_inc(yidx_in[par], 16)

            with sp.Fori(0, 4) as i:
                y_store(i)
            y_store(4, last=True)
            for par in range(2):
                sp.wait_ge(y_out[par], 80)
            sp.wait_ge(y_zero, 16)

            def load1(c, par, ck):
                sp.wait_ge(rows_done, EDGE0 + (ck - 1) * OC)
                src_load(c, par, s1_in)
                sp.wait_ge(v_done, EDGE0 + (ck - 1) * OC)
                first = sp.value_load(base_i[0:1, bass.ds(ck, 1)], min_val=0, max_val=NODES - 1)
                sp.dma_start(ywin[:, par, :], y_tab[bass.ds(first, P), :]).then_inc(ywin_in[par], 16)

            with sp.If(flag > 0):
                with sp.Fori(0, PAIRS) as i:
                    for par in range(2):
                        load1(i * 2 + par, par, i * 2 + par)
                load1(None, 0, FULL)
            with sp.Else():
                tiles(sp, lambda t, last: g_load(BATON1 + t * STEPS1, t, last, False))
            sp.wait_ge(acc_done, 1)
            for half in range(2):
                if half:
                    sp.wait_ge(acc_used, 1)
                for k in range(4):
                    a = 4 * half + k
                    sp.dma_start(gates[:, :, NC * k:NC * (k + 1)], acc[a][0:NODES, :].rearrange(
                        "(p j) f -> p j f", j=NJ)).then_inc(acc_in, 16)
            sp.wait_ge(result, 1)
            sp.dma_start(out.rearrange("(p j) f -> p j f", j=NJ), xs[:, :, :]).then_inc(out_done, 16)
            sp.wait_ge(out_done, 16)
            sp.wait_ge(table, 16 * (REPEATS + 1))
            sp.wait_ge(x2_out, 16)

        @block.gpsimd
        def _(pool):
            pool.memset(w1bd[:, :], 0.0).then_inc(w1_zero, 1)
            pool.memset(wc[:, :], 0.0).then_inc(wc_zero, 1)
            pool.memset(zeros[:, :], 0.0).then_inc(consts, 1)
            pool.memset(ident[:, :], 1.0).then_inc(consts, 1)
            pool.memset(before[:, :], 1.0).then_inc(consts, 1)
            pool.iota(cols[:, :], [[1, P]], base=0, channel_multiplier=0,
                      allow_small_or_imprecise_dtypes=True).then_inc(consts, 1)
            pool.iota(part[:, :], [[0, 1]], base=0, channel_multiplier=1,
                      allow_small_or_imprecise_dtypes=True).then_inc(consts, 1)
            pool.iota(dummy[:, :], [[0, 1]], base=NODES, channel_multiplier=1,
                      allow_small_or_imprecise_dtypes=True).then_inc(consts, 1)
            pool.wait_ge(consts, 6)
            pool.affine_select(out=ident[:, :], in_=ident[:, :], pattern=[[-1, P]], compare_op=ALU.is_equal,
                               fill=0.0, base=0, channel_multiplier=1).then_inc(consts, 1)
            pool.affine_select(out=before[:, :], in_=before[:, :], pattern=[[-1, P]], compare_op=ALU.is_gt,
                               fill=0.0, base=0, channel_multiplier=1).then_inc(consts, 1)
            pool.wait_ge(prep, PREP_SPAN)
            pool.partition_all_reduce(spanr[:, :, :].rearrange("p a c -> p (a c)"),
                                      span[:, :, :].rearrange("p a c -> p (a c)"), P,
                                      bass.bass_isa.ReduceOp.max).then_inc(spans_out, 1)
            pool.wait_ge(prep, PREP_REL)
            tail = dst_rel[:, FULL * G:]
            pool.affine_select(out=tail, in_=tail, pattern=[[1, OT]], compare_op=ALU.is_ge, fill=-1.0,
                               base=-DUP, channel_multiplier=OT).then_inc(masked, 1)

            def zero_agg():
                half = ROWS // 2
                for k in range(2):
                    pool.dma_start(agg[half * k:half * (k + 1), :].rearrange("(p r) f -> p (r f)", p=64),
                                 zeros[64 * k:64 * (k + 1), :]).then_inc(agg_rows, 16)

            for k in range(ACCS):
                pool.dma_start(acc[k].rearrange("(p r) f -> p (r f)", p=P), zeros[:, 0:ROWS * NC // P]
                             ).then_inc(acc_rows[k], 16)

            flag = fits(pool)

            def g_gather(n, at, tab, index):
                hold(pool, g_in, at)
                pool.indirect_dma_start(
                    out=g_x[:, :], out_offset=None, in_=tab,
                    in_offset=bass.IndirectOffsetOnAxis(ap=index[:, :], axis=0)).then_inc(g_gathered, 16)

            def g_scatter(step, tab, width, landed, count):
                hold(pool, baton, step + 1)
                pool.indirect_dma_start(
                    out=tab, out_offset=bass.IndirectOffsetOnAxis(ap=g_rows[:, :], axis=0),
                    in_=g_sum[:, 0:width], in_offset=None, compute_op=ALU.add).then_inc(landed, 16)
                hold(pool, landed, count)
                pool.sem_inc(baton, 1)

            with pool.Fori(0, REPEATS) as r:
                hold(pool, table, 16 * (r + 1))
                zero_agg()

                def add_window(ck, par):
                    hold(pool, win_out, 4 + 2 * (r * CHUNKS + ck) + 2)
                    hold(pool, agg_rows, ADDS * r + 16 * (ck + 2))
                    pool.indirect_dma_start(
                        out=agg, out_offset=bass.IndirectOffsetOnAxis(ap=win_rows[:, par:par + 1], axis=0),
                        in_=win[:, par, :], in_offset=None, compute_op=ALU.add).then_inc(agg_rows, 16)

                def gather(q, j, i):
                    if j % OC == 0:
                        hold(pool, src_in[j // OC % 2], 16 * (r * NCH[j // OC % 2] + i + 1))
                    hold(pool, prod_done, 4 * (r * OCTETS + q) + 4)
                    hold(pool, x_copied, r * OCTETS + q + 1)
                    for k in range(OT):
                        g = j % OC * OT + k
                        pool.indirect_dma_start(
                            out=xg[:, j, k, :], out_offset=None, in_=hx_tab,
                            in_offset=bass.IndirectOffsetOnAxis(ap=src_i[:, j // OC, g:g + 1], axis=0)
                        ).then_inc(gathered[j], 16)

                def turn(i, first=False):
                    for j in range(SIX):
                        gather(i * SIX + j, j, i)
                        if j == 1 and not first:
                            add_window(i * 2 - 1, 1)
                        if j == OC + 1:
                            add_window(i * 2, 0)

                def g_tile(t, last):
                    n = r * (TILES + 1) + t
                    g_gather(n, 48 * n + 48, hx_tab, g_src)
                    g_scatter(n * STEPS0 + 10, agg, GW, agg_rows, G_ADDS * r + 16 * t + 48)

                with pool.If(flag > 0):
                    turn(0, first=True)
                    with pool.Fori(1, PAIRS) as i:
                        turn(i)
                    gather(OCTETS - 1, 0, PAIRS)
                    add_window(FULL - 1, 1)
                    add_window(FULL, 0)
                    hold(pool, agg_rows, ADDS * (r + 1))
                with pool.Else():
                    hold(pool, agg_rows, G_ADDS * r + 32)
                    tiles(pool, g_tile)
                pool.sem_inc(sums_done, 1)

            pool.wait_ge(x2_out, 16)

            def y_gather(i, first=False):
                for par in range(2):
                    hold(pool, yidx_in[par], 16 * (i + 1))
                    if not first:
                        hold(pool, y_out[par], 16 * i)
                    for k in range(10):
                        pool.indirect_dma_start(
                            out=yg[:, par, k, :], out_offset=None, in_=x2_tab,
                            in_offset=bass.IndirectOffsetOnAxis(ap=yidx[:, par, k:k + 1], axis=0)
                        ).then_inc(y_in[par], 16)

            y_gather(0, first=True)
            with pool.Fori(1, 5) as i:
                y_gather(i)

            def scatter(q, slot):
                hold(pool, m_copied, q + 4)
                hold(pool, rows_done, EDGE0 + q + 1)
                for k in range(OT):
                    hold(pool, acc_rows[k], 16 * (q + 1))
                    if k == OT - 1:
                        pool.sem_inc(scattered, 1)
                    pool.indirect_dma_start(
                        out=acc[k], out_offset=bass.IndirectOffsetOnAxis(ap=rows[:, slot, k:k + 1], axis=0),
                        in_=merged[:, slot, k, :], in_offset=None, compute_op=ALU.add).then_inc(acc_rows[k], 16)

            def g_tile1(t, last):
                g_gather(t, 48 * REPEATS * (TILES + 1) + 32 * t + 32, y_tab, g_dst)
                g_scatter(BATON1 + t * STEPS1 + 5, acc[0], NC, acc_rows[0], 16 * t + 32)

            for par in range(2):
                pool.wait_ge(y_out[par], 80)
            with pool.If(flag > 0):
                with pool.Fori(0, PAIRS) as i:
                    for j in range(SIX):
                        scatter(i * SIX + j, j % 3)
                scatter(OCTETS - 1, 0)
                for k in range(ACCS):
                    pool.wait_ge(acc_rows[k], 16 * (OCTETS + 1))
            with pool.Else():
                for k in range(ACCS):
                    pool.wait_ge(acc_rows[k], 16)
                tiles(pool, g_tile1)
            pool.sem_inc(acc_done, 1)

        @block.tensor
        def _(pe):
            pe.wait_ge(weights, 16 * 20)
            pe.wait_ge(consts, 8)
            pe.matmul(bank[6][0:NC, 0:3 * NC], b2t[:, :], wiht[:, :], start=True, stop=True).then_inc(b2w, 1)
            pe.wait_ge(b2w, 2)

            flag = fits(pe)

            def g_merge(step, width):
                hold(pe, baton, step + 1)
                pe.transpose(bank[2][:, 0:P], g_key[:, 0:1].to_broadcast([P, P]), ident[:, :]).then_inc(baton, 1)
                hold(pe, baton, step + 3)
                pe.matmul(bank[5][:, 0:width], g_same[:, :], g_vals[:, 0:width], start=True, stop=True
                          ).then_inc(baton, 1)

            with pe.Fori(0, REPEATS) as r:
                hold(pe, table, 16 * (r + 1))

                def turn_ef(q, j, i):
                    par, ch = j % 2, j // OC % 2
                    if j % OC == 0:
                        hold(pe, ef_in[ch], 16 * (r * NCH[ch] + i + 1))
                    hold(pe, ef_copied, r * OCTETS + q + 1)
                    for b in range(2):
                        at = (j % OC * OT + 4 * b) * FD
                        mm = pe.transpose(bank[6][0:4 * FD, (2 * par + b) * P:(2 * par + b + 1) * P],
                                          ef_sb[:, ch, at:at + 4 * FD], ident[:, :])
                    mm.then_inc(ef_turned, 1)

                def hidden(q, j):
                    par = j % 2
                    hold(pe, ef_copied, HALF0 + r * OCTETS + q + 1)
                    hold(pe, h_done, r * OCTETS + q + 1)
                    pe.matmul(bank[7][:, 2 * par * P:2 * (par + 1) * P], w1bd[:, :], eft[:, par, :],
                              start=True, stop=True).then_inc(h_summed, 1)

                def edge_matrices(q, j, t):
                    hold(pe, prod_done, PROD0 + 4 * (r * OCTETS + q - 1) + t + 1)
                    for b in range(2):
                        mm = pe.matmul(bank[t][:, MW * b:MW * (b + 1)],
                                       ht[HID * t:HID * (t + 1), j % 2, P * b:P * (b + 1)],
                                       w2s[HID * t:HID * (t + 1), :], start=True, stop=True,
                                       tile_position=(HID * t, 0))
                    mm.then_inc(w_done, 1)

                def segment_sum(q, j, t, ck):
                    hold(pe, prod_done, PROD0 + 4 * (r * OCTETS + q) + t + 1)
                    if t == 0:
                        hold(pe, hot_done, r * OCTETS + q + 1)
                        hold(pe, x_copied, XC0 + r * OCTETS + q + 1)
                        if j % OC == 0:
                            hold(pe, win_out, 2 * (r * CHUNKS + ck) + 2)
                    only = isinstance(q, int) and q == OCTETS - 1
                    for b in range(2):
                        k = 4 * b + t
                        mm = pe.matmul(bank[4 + j // OC % 2][:, 0:AW], onehot[:, j % 2, k, :],
                                       prod[:, j % 2, k, :], start=(j % OC == 0 and t == 0 and b == 0),
                                       stop=((j % OC == OC - 1 or only) and t == 3 and b == 1))
                    if t == 3:
                        mm.then_inc(octet_summed, 1)

                def octet(q, j, i, ck, last=False):
                    if not last:
                        turn_ef(q + 1, (j + 1) % SIX, i if j < SIX - 1 else i + 1)
                    hold(pe, h_done, HALF0 + r * OCTETS + q + 1)
                    edge_matrices(q, j, 0)
                    edge_matrices(q, j, 1)
                    segment_sum(q, j, 0, ck)
                    edge_matrices(q, j, 2)
                    if not last:
                        hidden(q + 1, (j + 1) % SIX)
                    segment_sum(q, j, 1, ck)
                    edge_matrices(q, j, 3)
                    segment_sum(q, j, 2, ck)
                    segment_sum(q, j, 3, ck)

                def g_tile(t, last):
                    n = r * (TILES + 1) + t
                    step = n * STEPS0
                    hold(pe, g_in, 48 * n + 48)
                    pe.transpose(bank[6][0:FD, 0:P], g_ef[:, :], ident[:, :]).then_inc(baton, 1)
                    hold(pe, baton, step + 3)
                    pe.matmul(bank[7][0:HID, 0:P], w1bd[0:FD, 0:HID], eft[0:FD, 0, 0:P], start=True, stop=True
                              ).then_inc(baton, 1)
                    hold(pe, baton, step + 5)
                    pe.matmul(bank[0][:, 0:MW], ht[0:HID, 0, 0:P], w2s[0:HID, :], start=True, stop=True
                              ).then_inc(baton, 1)
                    g_merge(step + 6, GW)

                with pe.If(flag > 0):
                    turn_ef(0, 0, 0)
                    hidden(0, 0)
                    with pe.Fori(0, PAIRS) as i:
                        for j in range(SIX):
                            octet(i * SIX + j, j, i, i * 2 + j // OC)
                    octet(OCTETS - 1, 0, PAIRS, FULL, last=True)
                with pe.Else():
                    tiles(pe, g_tile)

                hold(pe, own, own_base(r) + 3)

                def turn_gin(u, par):
                    hold(pe, gin_copied, GU * r + u + 1)
                    hold(pe, gin_staged, GU * r + u + 1)
                    for k in range(GT):
                        mm = pe.transpose(bank[par][0:3 * NC + 2, NP_ * k:NP_ * (k + 1)],
                                          gin_four[:, par, k, :], ident[0:NP_, 0:NP_])
                    mm.then_inc(gin_turned, 1)

                def gate_sums(u, par):
                    hold(pe, gin_copied, GU * r + u + 3)
                    hold(pe, gate_copied, GU * r + u + 1)
                    for k in range(GT):
                        mm = pe.matmul(bank[2 + par][0:NP_, 4 * NC * k:4 * NC * (k + 1)],
                                       gint[:, par, NP_ * k:NP_ * (k + 1)], wc[:, :], start=True, stop=True)
                    mm.then_inc(gate_summed, 1)

                turn_gin(0, 0)
                with pe.Fori(0, GU // 2) as v:
                    turn_gin(v * 2 + 1, 1)
                    gate_sums(v * 2, 0)
                    turn_gin(v * 2 + 2, 0)
                    gate_sums(v * 2 + 1, 1)
                gate_sums(GU - 1, 0)

            pe.wait_ge(x2_out, 16)

            def octet1(q, j, i):
                par, ch = j % 2, j // OC % 2
                hold(pe, hot1, 2 * q + 2)
                for h in range(2):
                    hold(pe, same_done, 2 * q + h + 1)
                    for k in range(4):
                        mm = pe.transpose(bank[2 + h][:, P * k:P * (k + 1)],
                                          srcf[:, par, 4 * h + k:4 * h + k + 1].to_broadcast([P, P]), ident[:, :])
                    mm.then_inc(turned1, 1)
                for h in range(2):
                    hold(pe, oht_done, 2 * q + h + 1)
                    for k in range(4):
                        mm = pe.transpose(bank[h][:, P * k:P * (k + 1)], onehot[:, par, 4 * h + k, :], ident[:, :])
                    mm.then_inc(turned1, 1)
                if j % OC == 0:
                    hold(pe, ywin_in[ch], 16 * (i + 1))
                hold(pe, oht_done, 2 * q + 4)
                hold(pe, v_copied, q + 1)
                for k in range(OT):
                    mm = pe.matmul(bank[4][:, P * par + NC * k:P * par + NC * (k + 1)], oht[:, par, P * k:P * (k + 1)],
                                   ywin[:, ch, :], start=True, stop=True)
                mm.then_inc(v_done, 1)
                hold(pe, v_copied, q + 3)
                hold(pe, same_done, 2 * q + 4)
                hold(pe, m_copied, q + 2)
                for k in range(OT):
                    mm = pe.matmul(bank[5][:, P * par + NC * k:P * par + NC * (k + 1)], same[:, par, k, :],
                                   vals[:, par, k, :], start=True, stop=True)
                mm.then_inc(m_done, 1)

            with pe.If(flag > 0):
                with pe.Fori(0, PAIRS) as i:
                    for j in range(SIX):
                        octet1(i * SIX + j, j, i)
                octet1(OCTETS - 1, 0, PAIRS)
            with pe.Else():
                tiles(pe, lambda t, last: g_merge(BATON1 + t * STEPS1 + 1, NC))

        @block.scalar
        def _(act):
            act.sem_inc(ef_copied, HALF0)
            act.sem_inc(h_done, HALF0)
            act.sem_inc(x_copied, XC0)
            act.sem_inc(gin_copied, 2)
            act.sem_inc(oht_done, 2)
            act.sem_inc(v_copied, 2)
            act.sem_inc(m_copied, 3)
            act.wait_ge(b2w, 1)
            act.wait_ge(wc_zero, 1)
            act.copy(wc[0:NC, 0:3 * NC], bank[6][0:NC, 0:3 * NC]).then_inc(b2w, 1)

            flag = fits(act)

            with act.Fori(0, REPEATS) as r:
                hold(act, table, 16 * (r + 1))

                def octet(q, j, i):
                    par = j % 2
                    hold(act, ef_turned, EDGE0 + r * OCTETS + q + 1)
                    hold(act, h_summed, r * OCTETS + q + 1)
                    act.copy(eft[:, par, :], bank[6][0:4 * FD, 2 * par * P:2 * (par + 1) * P]).then_inc(ef_copied, 1)
                    hold(act, h_summed, HALF0 + r * OCTETS + q + 1)
                    hold(act, w_done, W0 + 4 * (r * OCTETS + q - 1))
                    act.activation(ht[:, par, :], bank[7][:, 2 * par * P:2 * (par + 1) * P], ACT.Relu,
                                   bias=b1c[:, 0:1]).then_inc(h_done, 1)
                    hold(act, gathered[j], 128 * (r * NSLOT[j] + i + 1))
                    hold(act, octet_summed, r * OCTETS + q + 1)
                    act.copy(prod[:, par, :, MW:MW + NC], xg[:, j, :, :]).then_inc(x_copied, 1)

                def g_tile(t, last):
                    step = (r * (TILES + 1) + t) * STEPS0
                    hold(act, baton, step + 2)
                    act.copy(eft[0:FD, 0, 0:P], bank[6][0:FD, 0:P]).then_inc(baton, 1)
                    hold(act, baton, step + 4)
                    act.activation(ht[0:HID, 0, 0:P], bank[7][0:HID, 0:P], ACT.Relu, bias=b1c[0:HID, 0:1]
                                   ).then_inc(baton, 1)

                with act.If(flag > 0):
                    with act.Fori(0, PAIRS) as i:
                        for j in range(SIX):
                            octet(i * SIX + j, j, i)
                    octet(OCTETS - 1, 0, PAIRS)
                with act.Else():
                    tiles(act, g_tile)

                def gin_copy(u, par):
                    hold(act, gin_turned, GU * r + u + 1)
                    hold(act, gate_summed, GU * r + u + 1)
                    act.copy(gint[:, par, :], bank[par][0:3 * NC + 2, 0:GT * NP_]).then_inc(gin_copied, 1)

                def gin_stage(u, par):
                    act.copy(gin_four[:, par, :, :], gin[:, bass.ds(u * GT, GT), :]).then_inc(gin_staged, 1)

                hold(act, own, own_base(r) + 3)
                gin_stage(0, 0)
                with act.Fori(0, GU // 2) as v:
                    for par in range(2):
                        gin_stage(v * 2 + par + 1, 1 - par)
                        gin_copy(v * 2 + par, par)
                gin_copy(GU - 1, 0)
                hold(act, gate_copied, GU * (r + 1) + 2)
                act.activation(gates[:, :, 0:2 * NC], gates[:, :, 0:2 * NC], ACT.Sigmoid).then_inc(act_gates, 1)
                hold(act, own, own_base(r) + 5)
                act.activation(gates[:, :, 2 * NC:3 * NC], gates[:, :, 2 * NC:3 * NC], ACT.Tanh
                               ).then_inc(act_gates, 1)

            def root(n):
                act.wait_ge(own, OWN_LN[n])
                act.activation(stat[:, 1, :], stat[:, 1, :], ACT.Sqrt).then_inc(ln_sqrt, 1)

            root(0)

            def octet1(q, j, slot):
                par = j % 2
                hold(act, v_done, q + 5)
                for h in range(2):
                    hold(act, turned1, 4 * q + 3 + h)
                    act.copy(oht[:, par, 4 * P * h:4 * P * (h + 1)], bank[h][:, :]).then_inc(oht_done, 1)
                hold(act, v_done, q + 7)
                hold(act, m_done, q + 1)
                act.copy(vals[:, par, :, :].rearrange("p k f -> p (k f)"), bank[4][:, P * par:P * (par + 1)]
                         ).then_inc(v_copied, 1)
                hold(act, m_done, q + 3)
                hold(act, scattered, q + 1)
                act.copy(merged[:, slot, :, :].rearrange("p k f -> p (k f)"), bank[5][:, P * par:P * (par + 1)]
                         ).then_inc(m_copied, 1)

            with act.If(flag > 0):
                with act.Fori(0, PAIRS) as i:
                    for j in range(SIX):
                        octet1(i * SIX + j, j, j % 3)
                octet1(OCTETS - 1, 0, 0)
            root(1)

        @block.vector
        def _(dve):
            dve.sem_inc(prod_done, PROD0)
            dve.sem_inc(win_out, 4)
            dve.sem_inc(gate_copied, 2)
            dve.sem_inc(same_done, 2)
            dve.sem_inc(rows_done, EDGE0)
            dve.sem_inc(ef_turned, EDGE0)
            dve.sem_inc(h_summed, HALF0)
            dve.sem_inc(w_done, W0)
            dve.sem_inc(octet_summed, 2)
            dve.sem_inc(gate_summed, 2)
            dve.sem_inc(v_done, EDGE0)
            dve.sem_inc(m_done, 2)
            dve.sem_inc(scattered, 2)
            dve.sem_inc(baton, 1)

            steps = [0]

            def step(ins):
                ins.then_inc(prep, 1)
                steps[0] += 1
                return steps[0]

            dve.wait_ge(dst_in, 48)
            n = step(dve.tensor_copy(dst_rel[:, :], dst_i[:, :]))
            dve.wait_ge(prep, n)
            full = dst_rel[:, 0:FULL * G].rearrange("p (c g) -> p c g", g=G)
            tail = dst_rel[:, FULL * G:]
            step(dve.tensor_reduce(span[:, 0, 0:FULL], full, AX, ALU.max))
            step(dve.tensor_reduce(span[:, 0, FULL:], tail, AX, ALU.max))
            step(dve.tensor_reduce(span[:, 1, 0:FULL], full, AX, ALU.min))
            n = step(dve.tensor_reduce(span[:, 1, FULL:], tail, AX, ALU.min))
            dve.wait_ge(prep, n)
            n = step(dve.tensor_scalar(span[:, 1, :], span[:, 1, :], -1.0, None, ALU.mult))
            assert n == PREP_SPAN
            dve.wait_ge(spans_out, 1)
            dve.wait_ge(consts, 6)
            step(dve.tensor_scalar(base_f[:, :], spanr[:, 1, :], -1.0, None, ALU.mult))
            n = step(dve.tensor_tensor(width[:, :], spanr[:, 0, :], spanr[:, 1, :], ALU.add))
            dve.wait_ge(prep, n)
            step(dve.tensor_copy(base_i[:, :], base_f[:, :]))
            step(dve.tensor_scalar(rows_i[:, :], base_f[:, :], part[:, 0:1], None, ALU.add))
            step(dve.tensor_reduce(widest[:, :], width[:, :], AX, ALU.max))
            step(dve.tensor_tensor(full, full, base_f[:, 0:FULL].unsqueeze(2).to_broadcast([P, FULL, G]),
                                   ALU.subtract))
            n = step(dve.tensor_scalar(tail, tail, base_f[:, FULL:], None, ALU.subtract))
            assert n == PREP_REL
            dve.wait_ge(prep, n)
            n = step(dve.tensor_scalar(windowed[:, :], widest[:, :], float(P), None, ALU.is_lt))
            assert n == PREP_FLAG
            step(dve.tensor_scalar(g_valid[:, :], part[:, 0:1], float(TDUP), None, ALU.is_ge))
            step(dve.memset(g_vals[:, 2 * NC:], 1.0))
            step(dve.memset(prod[:, :, :, MW + NC:], 1.0))
            n = step(dve.memset(gin[:, :, 3 * NC:], 1.0))
            step(dve.tensor_copy(gin[:, :, 2 * NC:3 * NC], xs[:, :, :]))
            dve.wait_ge(masked, 1)
            dve.wait_ge(prep, n + 1)

            flag = fits(dve)

            def g_after(ins, count):
                ins.then_inc(g_own, 1)
                hold(dve, g_own, count)

            def g_keys(step, own_at, index, last):
                if last:
                    g_after(dve.tensor_copy(g_away[:, :], index[:, :]), own_at + 1)
                    g_after(dve.tensor_tensor(g_away[:, :], g_away[:, :], dummy[:, :], ALU.subtract), own_at + 2)
                    dve.scalar_tensor_tensor(out=g_key[:, :], in0=g_away[:, :], scalar=g_valid[:, 0:1],
                                             in1=dummy[:, :], op0=ALU.mult, op1=ALU.add).then_inc(baton, 1)
                else:
                    dve.tensor_copy(g_key[:, :], index[:, :]).then_inc(baton, 1)

            def g_rows_of(step, own_at, width):
                hold(dve, baton, step + 1)
                dve.tensor_scalar(g_same[:, :], bank[2][:, 0:P], g_key[:, 0:1], None, ALU.is_equal).then_inc(baton, 1)
                hold(dve, baton, step + 3)
                g_after(dve.tensor_tensor(g_early[:, :], g_same[:, :], before[:, :], ALU.mult), own_at + 1)
                g_after(dve.tensor_reduce(g_count[:, :], g_early[:, :], AX, ALU.max), own_at + 2)
                g_after(dve.tensor_tensor(g_away[:, :], dummy[:, :], g_key[:, :], ALU.subtract), own_at + 3)
                g_after(dve.scalar_tensor_tensor(out=g_rows[:, :], in0=g_away[:, :], scalar=g_count[:, 0:1],
                                                 in1=g_key[:, :], op0=ALU.mult, op1=ALU.add), own_at + 4)
                dve.tensor_copy(g_sum[:, 0:width], bank[5][:, 0:width]).then_inc(baton, 1)

            with dve.Fori(0, REPEATS) as r:
                hold(dve, table, 16 * (r + 1))
                B = own_base(r)

                def after(ins, k):
                    ins.then_inc(own, 1)
                    dve.wait_ge(own, own_base(r) + k)

                def window_out(ck, par):
                    hold(dve, octet_summed, 2 + r * OCTETS + minimum(ck))
                    hold(dve, agg_rows, ADDS * r + 16 * (ck + 1))
                    dve.tensor_reduce(win[:, par, 0:NC], bank[4 + par][:, 0:MW].rearrange("p (i o) -> p o i", i=NC),
                                      AX, ALU.add)
                    dve.tensor_copy(win_rows[:, par:par + 1], rows_i[:, bass.ds(ck, 1)]).then_inc(win_out, 1)
                    dve.tensor_copy(win[:, par, NC:], bank[4 + par][:, MW:AW]).then_inc(win_out, 1)

                def minimum(ck):
                    return ck * OC + OC if not isinstance(ck, int) or ck < FULL else OCTETS

                def hots(q, par, last_sum):
                    dve.tensor_tensor(onehot[:, par, :, :], cols[:, :].unsqueeze(1).to_broadcast([P, OT, P]),
                                      dst_rel[:, bass.ds(q * OT, OT)].unsqueeze(2).to_broadcast([P, OT, P]),
                                      ALU.is_equal).then_inc(hot_done, 1)

                def octet(q, j, i, out_of=None):
                    par = j % 2
                    hold(dve, octet_summed, r * OCTETS + q + 1)
                    hots(q, par, None)
                    hold(dve, gathered[j], 128 * (r * NSLOT[j] + i + 1))
                    for t in range(4):
                        hold(dve, w_done, W0 + 4 * (r * OCTETS + q) + t + 1)
                        dve.tensor_tensor(
                            prod[:, par, t::4, 0:MW].rearrange("p b (i o) -> p b i o", i=NC),
                            bank[t][:, :].rearrange("p (b i o) -> p b i o", b=2, i=NC),
                            xg[:, j, t::4, :].unsqueeze(3).to_broadcast([P, 2, NC, NC]),
                            ALU.mult).then_inc(prod_done, 1)
                        if t == 1 and out_of is not None:
                            window_out(*out_of)

                def turn(i, first=False):
                    for j in range(SIX):
                        out_of = None
                        if j == 0 and not first:
                            out_of = (i * 2 - 1, 1)
                        if j == OC:
                            out_of = (i * 2, 0)
                        octet(i * SIX + j, j, i, out_of)

                def g_tile(t, last):
                    n = r * (TILES + 1) + t
                    step, own_at = n * STEPS0, n * 5 + r * 2
                    hold(dve, g_gathered, 16 * n + 16)
                    hold(dve, baton, step + 6)
                    g_after(dve.tensor_tensor(
                        g_prod[:, :].rearrange("p (i o) -> p i o", i=NC),
                        bank[0][:, 0:MW].rearrange("p (i o) -> p i o", i=NC),
                        g_x[:, :].unsqueeze(2).to_broadcast([P, NC, NC]), ALU.mult), own_at + 1)
                    dve.tensor_reduce(g_vals[:, 0:NC], g_prod[:, :].rearrange("p (i o) -> p o i", i=NC), AX, ALU.add)
                    dve.tensor_copy(g_vals[:, NC:2 * NC], g_x[:, :])
                    g_keys(step, own_at + 1, g_dst, last)
                    g_rows_of(step + 7, own_at + (3 if last else 1), GW)

                with dve.If(flag > 0):
                    turn(0, first=True)
                    with dve.Fori(1, PAIRS) as i:
                        turn(i)
                    octet(OCTETS - 1, 0, PAIRS, (FULL - 1, 1))
                    window_out(FULL, 0)
                with dve.Else():
                    tiles(dve, g_tile)

                hold(dve, agg_in, 16 * (r + 1))
                after(dve.tensor_scalar(inv[:, :], aggl[:, :, 2 * NC:].rearrange("p j a -> p (j a)"), 1.0, None,
                                        ALU.max), 1)
                dve.reciprocal(inv[:, :], inv[:, :]).then_inc(own, 1)
                hold(dve, own, own_base(r) + 2)
                spread = inv[:, :].unsqueeze(2).to_broadcast([NP_, NJ, NC])
                dve.tensor_tensor(gin[:, :, 0:NC], aggl[:, :, NC:2 * NC], spread, ALU.mult)
                dve.tensor_tensor(gin[:, :, NC:2 * NC], aggl[:, :, 0:NC], spread, ALU.mult).then_inc(own, 1)

                def gate_out(u, par):
                    hold(dve, gate_summed, GU * r + u + 3)
                    dve.tensor_copy(gates[:, bass.ds(u * GT, GT), :],
                                    bank[2 + par][0:NP_, 0:GT * 4 * NC].rearrange("p (k f) -> p k f", k=GT)
                                    ).then_inc(gate_copied, 1)

                with dve.Fori(0, GU // 2) as v:
                    for par in range(2):
                        gate_out(v * 2 + par, par)
                gate_out(GU - 1, 0)
                hold(dve, act_gates, 2 * r + 1)
                g_r, g_z, g_n, g_h = (gates[:, :, NC * k:NC * (k + 1)] for k in range(4))
                h = gin[:, :, 2 * NC:3 * NC]
                after(dve.tensor_tensor(g_h, g_h, g_r, ALU.mult), 4)
                dve.tensor_tensor(g_n, g_n, g_h, ALU.add).then_inc(own, 1)
                hold(dve, act_gates, 2 * r + 2)
                after(dve.tensor_tensor(g_r, h, g_n, ALU.subtract), 6)
                after(dve.tensor_tensor(g_r, g_r, g_z, ALU.mult), 7)
                after(dve.tensor_tensor(h, g_n, g_r, ALU.add), 8)

            done = [own_base(REPEATS)]

            def link(ins):
                ins.then_inc(own, 1)
                done[0] += 1
                dve.wait_ge(own, done[0])

            def layernorm(n):
                mean, var, tmp = stat[:, 0, :], stat[:, 1, :], stat[:, 2, :]
                wide = lambda v: v.unsqueeze(2).to_broadcast([NP_, NJ, NC])
                link(dve.tensor_reduce(tmp, xs[:, :, :], AX, ALU.add))
                link(dve.tensor_scalar(mean, tmp, 1.0 / NC, None, ALU.mult))
                link(dve.tensor_tensor(xs[:, :, :], xs[:, :, :], wide(mean), ALU.subtract))
                link(dve.tensor_tensor(gates[:, :, 0:NC], xs[:, :, :], xs[:, :, :], ALU.mult))
                link(dve.tensor_reduce(tmp, gates[:, :, 0:NC], AX, ALU.add))
                link(dve.tensor_scalar(var, tmp, 1.0 / NC, EPS, ALU.mult, ALU.add))
                assert done[0] == OWN_LN[n]
                dve.wait_ge(ln_sqrt, n + 1)
                link(dve.reciprocal(tmp, var))
                return dve.tensor_tensor(xs[:, :, :], xs[:, :, :], wide(tmp), ALU.mult)

            link(dve.tensor_tensor(xs[:, :, :], xs[:, :, :], gin[:, :, 2 * NC:3 * NC], ALU.add))
            link(layernorm(0))
            assert done[0] == OWN_X2

            dve.wait_ge(table, 16 * (REPEATS + 1))

            def octet1(q, j, i, slot):
                par, ch = j % 2, j // OC % 2
                if j % OC == 0:
                    hold(dve, s1_in[ch], 16 * (i + 1))
                hold(dve, m_done, q + 1)
                dve.tensor_tensor(onehot[:, par, :, :], cols[:, :].unsqueeze(1).to_broadcast([P, OT, P]),
                                  dst_rel[:, bass.ds(q * OT, OT)].unsqueeze(2).to_broadcast([P, OT, P]),
                                  ALU.is_equal).then_inc(hot1, 1)
                g = j % OC * OT
                dve.tensor_copy(srcf[:, par, :], src_i[:, ch, g:g + OT]).then_inc(hot1, 1)
                hold(dve, hot1, 2 * q + 2)
                dve.tensor_scalar(away[:, :], srcf[:, par, :], -1.0, dummy[:, 0:1], ALU.mult, ALU.add
                                  ).then_inc(own1, 1)
                for h in range(2):
                    hold(dve, turned1, 4 * q + h + 1)
                    dve.tensor_tensor(
                        same[:, par, 4 * h:4 * h + 4, :], bank[2 + h][:, :].rearrange("p (k e) -> p k e", k=4),
                        srcf[:, par, 4 * h:4 * h + 4].unsqueeze(2).to_broadcast([P, 4, P]), ALU.is_equal
                    ).then_inc(same_done, 1)
                hold(dve, same_done, 2 * q + 4)
                dve.tensor_tensor(earlier[:, :, :], same[:, par, :, :],
                                  before[:, :].unsqueeze(1).to_broadcast([P, OT, P]), ALU.mult).then_inc(own1, 1)
                hold(dve, own1, 5 * q + 2)
                dve.tensor_reduce(count[:, :], earlier[:, :, :], AX, ALU.add).then_inc(own1, 1)
                hold(dve, own1, 5 * q + 3)
                dve.tensor_scalar(count[:, :], count[:, :], 1.0, None, ALU.min).then_inc(own1, 1)
                hold(dve, own1, 5 * q + 4)
                dve.tensor_tensor(shift[:, :], count[:, :], away[:, :], ALU.mult).then_inc(own1, 1)
                hold(dve, own1, 5 * q + 5)
                hold(dve, scattered, q + 1)
                dve.tensor_tensor(rows[:, slot, :], srcf[:, par, :], shift[:, :], ALU.add).then_inc(rows_done, 1)

            def g_tile1(t, last):
                step, own_at = BATON1 + t * STEPS1, REPEATS * (5 * (TILES + 1) + 2) + 4 * t
                hold(dve, g_gathered, 16 * (REPEATS * (TILES + 1) + t + 1))
                dve.tensor_copy(g_vals[:, 0:NC], g_x[:, :])
                g_keys(step, own_at, g_src, last)
                g_rows_of(step + 2, own_at + (2 if last else 0), NC)

            with dve.If(flag > 0):
                with dve.Fori(0, PAIRS) as i:
                    for j in range(SIX):
                        octet1(i * SIX + j, j, i, j % 3)
                octet1(OCTETS - 1, 0, PAIRS, 0)
            with dve.Else():
                tiles(dve, g_tile1)

            for half in range(2):
                dve.wait_ge(acc_in, 64 * (half + 1))
                for k in range(4):
                    link(dve.tensor_tensor(xs[:, :, :], xs[:, :, :], gates[:, :, NC * k:NC * (k + 1)], ALU.add))
                if half == 0:
                    dve.sem_inc(acc_used, 1)
            layernorm(1).then_inc(result, 1)


PREP_SPAN, PREP_REL, PREP_FLAG = 6, 13, 14


def own_base(r):
    return r * 8


OWN_X2 = own_base(REPEATS) + 9
OWN_LN = [own_base(REPEATS) + 7, OWN_X2 + 8 + 6]
STEPS0, STEPS1 = 11, 6
BATON1 = REPEATS * (TILES + 1) * STEPS0
G_ADDS = 16 * (2 + TILES + 1)

_INS = ['x', 'src', 'dst', 'edge_attr_13', 'L0_gnn_fnet_w1', 'L0_gnn_fnet_b1', 'L0_gnn_fnet_w2', 'L0_gnn_fnet_b2',
        'L0_gnn_gru_w_ih', 'L0_gnn_gru_w_hh', 'L0_gnn_gru_b_ih', 'L0_gnn_gru_b_hh']


def kernel(**inputs):
    import numpy as np
    import concourse.bacc as bacc
    from concourse import mybir
    from concourse.bass_utils import run_bass_kernel_spmd

    nc = bacc.Bacc("TRN2", target_bir_lowering=False, num_devices=1)
    arrays, args = {}, []
    for name in _INS:
        a = np.ascontiguousarray(inputs[name])
        arrays[f"in_{name}"] = a
        args.append(nc.dram_tensor(f"in_{name}", a.shape, mybir.dt.from_np(a.dtype), kind="ExternalInput").ap())
    args.append(nc.dram_tensor("out_0", (NODES, NC), mybir.dt.float32, kind="ExternalOutput").ap())
    program(nc, *args)
    run = run_bass_kernel_spmd(nc, [arrays], core_ids=[0])
    return run.results[0]["out_0"]
```

```python
from contextlib import ExitStack

import concourse.bass as bass
from concourse import mybir
from concourse.alu_op_type import AluOpType as ALU

F32 = mybir.dt.float32
I32 = mybir.dt.int32
BF16 = mybir.dt.bfloat16
ACT = mybir.ActivationFunctionType
AX = mybir.AxisListType.X

P = 128
NODES, NC = 12500, 16
EDGES, FD = 412500, 13
HID = 32
REPEATS = 2
OT = 8
G = 24
OC = G // OT
CE = P * G
FULL = EDGES // CE
CHUNKS = FULL + 1
TE = P * OT
PAIRS = FULL // 2
SIX = 2 * OC
OCTETS = FULL * OC + 1
DUP = TE - (EDGES - FULL * CE)
assert FULL % 2 == 0 and 0 <= DUP and G % OT == 0
NP_, NJ = 125, 100
ROWS = 99 * P
MW = NC * NC
HW = MW // 2
AW = NC + 1 + HW
GW = 2 * NC + 1
GT = 4
GU = NJ // GT
ACCS = 8
EPS = 1e-5
TILES = EDGES // P
TDUP = P - EDGES % P
TURN = 6
assert EDGES % P and TDUP > 0 and TILES % TURN == 0

PROD0, XC0, HALF0, W0, EDGE0 = 4 * SIX, SIX, 2, 8, SIX


def program(nc, x, src, dst, ef, w1, b1, w2, b2, wih, whh, bih, bhh, out):
    with ExitStack() as ctx:
        def sb(name, shape, dt=F32):
            return ctx.enter_context(nc.sbuf_tensor(name, shape, dt))

        def sem(name):
            return ctx.enter_context(nc.semaphore(name))

        def hold(eng, s, value):
            eng.wait_ge(s, value)
            eng.nop(nofuse=True)

        hx_tab = nc.dram_tensor("hx_tab", [NODES, NC], F32).ap()
        agg = nc.dram_tensor("agg", [ROWS, GW], F32).ap()
        x2_tab = nc.dram_tensor("x2_tab", [NODES, NC], F32).ap()
        y_tab = nc.dram_tensor("y_tab", [ROWS, NC], F32).ap()
        acc = [nc.dram_tensor(f"acc{k}", [ROWS, NC], F32).ap() for k in range(ACCS)]

        ident = sb("ident", [P, P])
        before = sb("before", [P, P])
        cols = sb("col_no", [P, P])
        part = sb("part_no", [P, 1])
        dummy = sb("spare", [P, 1])
        zeros = sb("zeros", [P, ROWS * GW // P])
        w1bd = sb("w1bd", [4 * FD, 4 * HID])
        b1c = sb("b1c", [P, 1])
        w2s = sb("w2s", [P, MW])
        wc = sb("wc", [3 * NC + 2, 4 * NC])
        b2t = sb("b2t", [NC, NC])
        wiht = sb("wiht", [NC, 3 * NC])

        dst_i = sb("dst_i", [P, OCTETS * OT], I32)
        dst_rel = sb("dst_rel", [P, OCTETS * OT])
        span = sb("span", [P, 2, CHUNKS])
        spanr = sb("spanr", [P, 2, CHUNKS])
        width = sb("width", [P, CHUNKS])
        base_f = sb("base_f", [P, CHUNKS])
        base_i = sb("base_i", [P, CHUNKS], I32)
        moved = sb("moved", [P, CHUNKS])
        carry_to = sb("carry_to", [P, CHUNKS])
        ordered = sb("ordered", [P, 1])
        widest = sb("widest", [P, 1])
        windowed = sb("windowed", [P, 1], I32)

        src_i = sb("src_i", [P, 2, G], I32)
        ef_sb = sb("ef_sb", [P, 2, G * FD])
        eft = sb("eft", [4 * FD, 2, 2 * P])
        ht = sb("ht", [P, 2, 2 * P])
        xg = sb("xg", [P, SIX, OT, NC])
        onehot = sb("onehot", [P, 2, OT, P])
        prod = sb("prod", [P, 4, 2, MW])
        terms = sb("terms", [P, 2, OT, AW])
        win = sb("win", [P, 2, GW])
        carry = sb("carry", [P, 2, P])

        xs = sb("xs", [NP_, NJ, NC])
        aggl = sb("aggl", [NP_, NJ, GW])
        gin = sb("gin", [NP_, NJ, 3 * NC + 2])
        gin_four = sb("gin_four", [NP_, 2, GT, 3 * NC + 2])
        gint = sb("gint", [3 * NC + 2, 2, GT * NP_])
        gates = sb("gates", [NP_, NJ, 4 * NC])
        inv = sb("inv", [NP_, NJ])
        stat = sb("stat", [NP_, 3, NJ])

        yidx = sb("yidx", [NP_, 2, 10], I32)
        yg = sb("yg", [NP_, 2, 10, NC])
        ywin = sb("ywin", [P, 2, NC])
        hot = sb("hot", [P, 2, OT, P], BF16)
        srcf = sb("srcf", [P, 2, OT])
        src_low = sb("src_low", [P, 2, OT], I32)
        src_lo = sb("src_lo", [P, 2, OT], BF16)
        src_hi = sb("src_hi", [P, 2, OT], BF16)
        ident_b = sb("ident_b", [P, P], BF16)
        oht = sb("oht", [P, 2, OT * P])
        same = sb("same", [P, 2, OT, P])
        earlier = sb("earlier", [P, OT, P])
        count = sb("count", [P, OT])
        away = sb("away", [P, OT])
        shift = sb("shift", [P, OT])
        vals = sb("vals", [P, 2, OT, NC])
        merged = sb("merged", [P, 3, OT, NC])
        rows = sb("rows", [P, 3, OT], I32)

        bank = [ctx.enter_context(nc.psum_tensor(f"bank{k}", [P, 512], F32)) for k in range(8)]

        g_src = sb("g_src", [P, 1], I32)
        g_dst = sb("g_dst", [P, 1], I32)
        g_ef = sb("g_ef", [P, FD])
        g_x = sb("g_x", [P, NC])
        g_prod = sb("g_prod", [P, MW])
        g_vals = sb("g_vals", [P, GW])
        g_key = sb("g_key", [P, 1])
        g_valid = sb("g_valid", [P, 1])
        g_same = sb("g_same", [P, P])
        g_early = sb("g_early", [P, P])
        g_count = sb("g_count", [P, 1])
        g_away = sb("g_away", [P, 1])
        g_rows = sb("g_rows", [P, 1], I32)
        g_sum = sb("g_sum", [P, GW])

        consts = sem("consts")
        weights = sem("weights")
        w1_zero = sem("w1_zero")
        wc_zero = sem("wc_zero")
        dst_in = sem("dst_in")
        prep = sem("prep")
        spans_out = sem("spans_out")
        masked = sem("masked")
        b2w = sem("b2w")
        table = sem("table")
        src_in = [sem(f"src_in{k}") for k in range(2)]
        ef_in = [sem(f"ef_in{k}") for k in range(2)]
        ef_turned = sem("ef_turned")
        ef_copied = sem("ef_copied")
        h_summed = sem("h_summed")
        h_done = sem("h_done")
        w_done = sem("w_done")
        gathered = [sem(f"gathered{k}") for k in range(SIX)]
        prod_done = sem("prod_done")
        half_done = sem("half_done")
        x_copied = sem("x_copied")
        hot_done = sem("hot_done")
        octet_summed = sem("octet_summed")
        win_out = sem("win_out")
        carry_done = sem("carry_done")
        agg_zero = sem("agg_zero")
        agg_rows = sem("agg_rows")
        agg_in = sem("agg_in")
        gin_done = sem("gin_done")
        gin_staged = sem("gin_staged")
        gin_turned = sem("gin_turned")
        gin_copied = sem("gin_copied")
        gate_summed = sem("gate_summed")
        gate_copied = sem("gate_copied")
        act_gates = sem("act_gates")
        own = sem("own")
        own1 = sem("own1")
        own_hot = sem("own_hot")
        x2_out = sem("x2_out")
        ln_sqrt = sem("ln_sqrt")
        y_zero = sem("y_zero")
        yidx_in = [sem(f"yidx_in{k}") for k in range(2)]
        y_in = [sem(f"y_in{k}") for k in range(2)]
        y_out = [sem(f"y_out{k}") for k in range(2)]
        ywin_in = [sem(f"ywin_in{k}") for k in range(2)]
        s1_in = [sem(f"s1_in{k}") for k in range(2)]
        hot1 = sem("hot1")
        turned1 = sem("turned1")
        oht_done = sem("oht_done")
        same_done = sem("same_done")
        rows_done = sem("rows_done")
        v_done = sem("v_done")
        v_copied = sem("v_copied")
        m_done = sem("m_done")
        m_copied = sem("m_copied")
        acc_rows = [sem(f"acc_rows{k}") for k in range(ACCS)]
        scattered = sem("scattered")
        acc_in = sem("acc_in")
        acc_used = sem("acc_used")
        result = sem("result")
        out_done = sem("out_done")

        sums_done = sem("sums_done")
        acc_done = sem("acc_done")
        baton = sem("baton")
        g_in = sem("g_in")
        g_gathered = [sem(f"g_gathered{j}") for j in range(TURN)]
        g_landed = [sem(f"g_landed{j}") for j in range(TURN)]
        g_own = sem("g_own")

        block = ctx.enter_context(nc.Block())

        def fits(eng):
            eng.wait_ge(prep, PREP_FLAG)
            return eng.value_load(windowed[0:1, 0:1], min_val=0, max_val=1)

        def tiles(eng, tile):
            with eng.Fori(0, TILES // TURN) as i:
                for j in range(TURN):
                    tile(i * TURN + j, False, i, j)
            tile(TILES, True, TILES // TURN, 0)

        def g_uses(run, i, j):
            return run * (TILES // TURN + (j == 0)) + i + 1

        NSLOT = [PAIRS + 1] + [PAIRS] * (SIX - 1)
        NCH = [PAIRS + 1, PAIRS]
        SRC_FULL = src[0:FULL * CE].rearrange("(c p g) -> c p g", p=P, g=G)
        EF_FULL = ef[0:FULL * CE, :].rearrange("(c p g) f -> c p (g f)", p=P, g=G)
        SRC_TAIL = src[EDGES - TE:EDGES].rearrange("(p g) -> p g", g=OT)
        EF_TAIL = ef[EDGES - TE:EDGES, :].rearrange("(p g) f -> p (g f)", g=OT)

        @block.sync
        def _(sp):
            def src_load(c, par, ring_in):
                if c is None:
                    sp.dma_start(src_i[:, par, 0:OT], SRC_TAIL).then_inc(ring_in[par], 16)
                else:
                    sp.dma_start(src_i[:, par, :], SRC_FULL[bass.ds(c, 1), :, :].rearrange("a p g -> (a p) g")
                                 ).then_inc(ring_in[par], 16)

            sp.dma_start(dst_i[:, 0:FULL * G].rearrange("p (c g) -> p c g", g=G),
                         dst[0:FULL * CE].rearrange("(c p g) -> p c g", p=P, g=G)).then_inc(dst_in, 16)
            sp.dma_start(dst_i[:, FULL * G:], dst[EDGES - TE:EDGES].rearrange("(p g) -> p g", g=OT)
                         ).then_inc(dst_in, 16)
            sp.dma_start(hx_tab, x).then_inc(table, 16)
            sp.dma_start(xs[:, :, :], x.rearrange("(p j) f -> p j f", j=NJ)).then_inc(dst_in, 16)
            sp.wait_ge(w1_zero, 1)
            for k in range(4):
                sp.dma_start(w1bd[FD * k:FD * (k + 1), HID * k:HID * (k + 1)], w1).then_inc(weights, 16)
                sp.dma_start(b1c[HID * k:HID * (k + 1), :], b1.rearrange("(k a) -> k a", a=1)).then_inc(weights, 16)
                sp.dma_start(w2s[HID * k:HID * (k + 1), :], w2).then_inc(weights, 16)
            sp.wait_ge(wc_zero, 1)
            with nc.allow_non_contiguous_dma(reason="768 weights, once"):
                sp.dma_start(wiht[:, :], wih.rearrange("o i -> i o")).then_inc(weights, 16)
                sp.dma_start(b2t[:, :], b2.rearrange("(i o) -> o i", o=NC)).then_inc(weights, 16)
                sp.dma_start(wc[NC:2 * NC, 0:3 * NC], wih.rearrange("o i -> i o")).then_inc(weights, 16)
                sp.dma_start(wc[2 * NC:3 * NC, 0:2 * NC], whh[0:2 * NC, :].rearrange("o i -> i o")
                             ).then_inc(weights, 16)
                sp.dma_start(wc[2 * NC:3 * NC, 3 * NC:4 * NC], whh[2 * NC:3 * NC, :].rearrange("o i -> i o")
                             ).then_inc(weights, 16)
            brow = lambda v: v.rearrange("(a k) -> a k", a=1)
            sp.dma_start(wc[3 * NC:3 * NC + 1, 0:3 * NC], brow(bih)).then_inc(weights, 16)
            sp.dma_start(wc[3 * NC + 1:3 * NC + 2, 0:2 * NC], brow(bhh[0:2 * NC])).then_inc(weights, 16)
            sp.dma_start(wc[3 * NC + 1:3 * NC + 2, 3 * NC:4 * NC], brow(bhh[2 * NC:3 * NC])).then_inc(weights, 16)
            sp.wait_ge(consts, 1)

            sp.dma_start(y_tab[NODES:ROWS, :].rearrange("(p r) f -> p (r f)", p=86), zeros[0:86, 0:2 * NC]
                         ).then_inc(y_zero, 16)

            flag = fits(sp)

            def g_load(first_step, t, last, attributes):
                hold(sp, baton, first_step + 1)
                e = EDGES - P if last else t * P
                sp.dma_start(g_src[:, :], src[bass.ds(e, P)].rearrange("(p a) -> p a", a=1)).then_inc(g_in, 16)
                sp.dma_start(g_dst[:, :], dst[bass.ds(e, P)].rearrange("(p a) -> p a", a=1)).then_inc(g_in, 16)
                if attributes:
                    sp.dma_start(g_ef[:, :], ef[bass.ds(e, P), :]).then_inc(g_in, 16)

            with sp.Fori(0, REPEATS) as r:
                sp.dma_start(agg.rearrange("(p r) f -> p (r f)", p=P), zeros[:, :]).then_inc(agg_zero, 16)
                hold(sp, agg_zero, 16 * (r + 1))

                def load0(c, par, ck):
                    hold(sp, ef_turned, EDGE0 + r * OCTETS + (ck - 1) * OC)
                    if c is None:
                        sp.dma_start(ef_sb[:, par, 0:OT * FD], EF_TAIL).then_inc(ef_in[par], 16)
                    else:
                        sp.dma_start(ef_sb[:, par, :], EF_FULL[bass.ds(c, 1), :, :].rearrange("a p g -> (a p) g")
                                     ).then_inc(ef_in[par], 16)
                    hold(sp, prod_done, PROD0 + (r * OCTETS + (ck - 1) * OC) * 4)
                    src_load(c, par, src_in)

                def store_window(c, par):
                    hold(sp, win_out, 4 + 2 * (r * CHUNKS + c) + 2)
                    hold(sp, agg_rows, 16 * (r * CHUNKS + c + 2))
                    first = sp.value_load(base_i[0:1, bass.ds(c, 1)], min_val=0, max_val=NODES - 1)
                    sp.dma_start(agg[bass.ds(first, P), :], win[:, par, :]).then_inc(agg_rows, 16)

                with sp.If(flag > 0):
                    for par in range(2):
                        load0(par, par, par)
                    with sp.Fori(1, PAIRS) as i:
                        for par in range(2):
                            load0(i * 2 + par, par, i * 2 + par)
                            store_window(i * 2 + par - 2, par)
                    load0(None, 0, FULL)
                    store_window(FULL - 2, 0)
                    store_window(FULL - 1, 1)
                    store_window(FULL, 0)
                    hold(sp, agg_rows, 16 * (r + 1) * CHUNKS + 32)
                with sp.Else():
                    tiles(sp, lambda t, last, i, j: g_load((r * (TILES + 1) + t) * STEPS0, t, last, True))
                    hold(sp, sums_done, r + 1)
                sp.dma_start(aggl[:, :, :], agg[0:NODES, :].rearrange("(p j) f -> p j f", j=NJ)).then_inc(agg_in, 16)
                hold(sp, own, own_base(r + 1))
                sp.dma_start(hx_tab.rearrange("(p j) f -> p j f", j=NJ), gin[:, :, 2 * NC:3 * NC]).then_inc(table, 16)
            hold(sp, own, OWN_X2)
            sp.dma_start(x2_tab.rearrange("(p j) f -> p j f", j=NJ), xs[:, :, :]).then_inc(x2_out, 16)

            YI = dst[0:NODES].rearrange("(p b k) -> b p k", p=NP_, k=10)
            YO = y_tab[0:NODES, :].rearrange("(p b k) f -> b p (k f)", p=NP_, k=10)
            for par in range(2):
                sp.dma_start(yidx[:, par, :], YI[par]).then_inc(yidx_in[par], 16)
            def y_store(i, last=False):
                for par in range(2):
                    hold(sp, y_in[par], 160 * (i + 1))
                    sp.dma_start(YO[bass.ds(i * 2 + par, 1), :, :].rearrange("a p k -> (a p) k"),
                                 yg[:, par, :, :].rearrange("p k f -> p (k f)")).then_inc(y_out[par], 16)
                    if not last:
                        sp.dma_start(yidx[:, par, :], YI[bass.ds(i * 2 + par + 2, 1), :, :].rearrange(
                            "a p k -> (a p) k")).then_inc(yidx_in[par], 16)

            with sp.Fori(0, 4) as i:
                y_store(i)
            y_store(4, last=True)
            for par in range(2):
                hold(sp, y_out[par], 80)
            hold(sp, y_zero, 16)

            def load1(c, par, ck):
                hold(sp, rows_done, EDGE0 + (ck - 1) * OC)
                src_load(c, par, s1_in)
                hold(sp, v_done, EDGE0 + (ck - 1) * OC)
                first = sp.value_load(base_i[0:1, bass.ds(ck, 1)], min_val=0, max_val=NODES - 1)
                sp.dma_start(ywin[:, par, :], y_tab[bass.ds(first, P), :]).then_inc(ywin_in[par], 16)

            with sp.If(flag > 0):
                with sp.Fori(0, PAIRS) as i:
                    for par in range(2):
                        load1(i * 2 + par, par, i * 2 + par)
                load1(None, 0, FULL)
            with sp.Else():
                tiles(sp, lambda t, last, i, j: g_load(BATON1 + t * STEPS1, t, last, False))
            hold(sp, acc_done, 1)
            for half in range(2):
                if half:
                    hold(sp, acc_used, 1)
                for k in range(4):
                    a = 4 * half + k
                    sp.dma_start(gates[:, :, NC * k:NC * (k + 1)], acc[a][0:NODES, :].rearrange(
                        "(p j) f -> p j f", j=NJ)).then_inc(acc_in, 16)
            hold(sp, result, 1)
            sp.dma_start(out.rearrange("(p j) f -> p j f", j=NJ), xs[:, :, :]).then_inc(out_done, 16)
            hold(sp, out_done, 16)
            hold(sp, table, 16 * (REPEATS + 1))
            hold(sp, x2_out, 16)

        @block.gpsimd
        def _(pool):
            pool.memset(w1bd[:, :], 0.0).then_inc(w1_zero, 1)
            pool.memset(wc[:, :], 0.0).then_inc(wc_zero, 1)
            pool.memset(zeros[:, :], 0.0).then_inc(consts, 1)
            pool.memset(ident[:, :], 1.0).then_inc(consts, 1)
            pool.memset(before[:, :], 1.0).then_inc(consts, 1)
            pool.iota(cols[:, :], [[1, P]], base=0, channel_multiplier=0,
                      allow_small_or_imprecise_dtypes=True).then_inc(consts, 1)
            pool.iota(part[:, :], [[0, 1]], base=0, channel_multiplier=1,
                      allow_small_or_imprecise_dtypes=True).then_inc(consts, 1)
            pool.iota(dummy[:, :], [[0, 1]], base=NODES, channel_multiplier=1,
                      allow_small_or_imprecise_dtypes=True).then_inc(consts, 1)
            pool.wait_ge(consts, 6)
            pool.affine_select(out=ident[:, :], in_=ident[:, :], pattern=[[-1, P]], compare_op=ALU.is_equal,
                               fill=0.0, base=0, channel_multiplier=1).then_inc(consts, 1)
            pool.affine_select(out=before[:, :], in_=before[:, :], pattern=[[-1, P]], compare_op=ALU.is_gt,
                               fill=0.0, base=0, channel_multiplier=1).then_inc(consts, 1)
            pool.wait_ge(prep, PREP_SPAN)
            pool.partition_all_reduce(spanr[:, :, :].rearrange("p a c -> p (a c)"),
                                      span[:, :, :].rearrange("p a c -> p (a c)"), P,
                                      bass.bass_isa.ReduceOp.max).then_inc(spans_out, 1)
            pool.wait_ge(prep, PREP_REL)
            tail = dst_rel[:, FULL * G:]
            pool.affine_select(out=tail, in_=tail, pattern=[[1, OT]], compare_op=ALU.is_ge, fill=-1.0,
                               base=-DUP, channel_multiplier=OT).then_inc(masked, 1)

            for k in range(ACCS):
                pool.dma_start(acc[k].rearrange("(p r) f -> p (r f)", p=P), zeros[:, 0:ROWS * NC // P]
                             ).then_inc(acc_rows[k], 16)

            flag = fits(pool)

            def g_gather(j, at, tab, index):
                hold(pool, g_in, at)
                pool.indirect_dma_start(
                    out=g_x[:, :], out_offset=None, in_=tab,
                    in_offset=bass.IndirectOffsetOnAxis(ap=index[:, :], axis=0)).then_inc(g_gathered[j], 16)

            def g_scatter(step, tab, width, j, uses):
                hold(pool, baton, step + 1)
                pool.indirect_dma_start(
                    out=tab, out_offset=bass.IndirectOffsetOnAxis(ap=g_rows[:, :], axis=0),
                    in_=g_sum[:, 0:width], in_offset=None, compute_op=ALU.add).then_inc(g_landed[j], 16)
                hold(pool, g_landed[j], 16 * uses)
                pool.sem_inc(baton, 1)

            with pool.Fori(0, REPEATS) as r:
                hold(pool, table, 16 * (r + 1))

                def gather(q, j, i):
                    if j % OC == 0:
                        hold(pool, src_in[j // OC % 2], 16 * (r * NCH[j // OC % 2] + i + 1))
                    hold(pool, prod_done, 4 * (r * OCTETS + q) + 4)
                    hold(pool, x_copied, r * OCTETS + q + 1)
                    for k in range(OT):
                        g = j % OC * OT + k
                        pool.indirect_dma_start(
                            out=xg[:, j, k, :], out_offset=None, in_=hx_tab,
                            in_offset=bass.IndirectOffsetOnAxis(ap=src_i[:, j // OC, g:g + 1], axis=0)
                        ).then_inc(gathered[j], 16)

                def g_tile(t, last, i, j):
                    n = r * (TILES + 1) + t
                    g_gather(j, 48 * n + 48, hx_tab, g_src)
                    g_scatter(n * STEPS0 + 10, agg, GW, j, g_uses(r, i, j))

                with pool.If(flag > 0):
                    with pool.Fori(0, PAIRS) as i:
                        for j in range(SIX):
                            gather(i * SIX + j, j, i)
                    gather(OCTETS - 1, 0, PAIRS)
                with pool.Else():
                    hold(pool, agg_zero, 16 * (r + 1))
                    tiles(pool, g_tile)
                    pool.sem_inc(sums_done, 1)

            pool.wait_ge(x2_out, 16)

            def y_gather(i, first=False):
                for par in range(2):
                    hold(pool, yidx_in[par], 16 * (i + 1))
                    if not first:
                        hold(pool, y_out[par], 16 * i)
                    for k in range(10):
                        pool.indirect_dma_start(
                            out=yg[:, par, k, :], out_offset=None, in_=x2_tab,
                            in_offset=bass.IndirectOffsetOnAxis(ap=yidx[:, par, k:k + 1], axis=0)
                        ).then_inc(y_in[par], 16)

            y_gather(0, first=True)
            with pool.Fori(1, 5) as i:
                y_gather(i)

            def scatter(q, slot):
                hold(pool, m_copied, q + 4)
                hold(pool, rows_done, EDGE0 + q + 1)
                for k in range(OT):
                    hold(pool, acc_rows[k], 16 * (q + 1))
                    if k == OT - 1:
                        pool.sem_inc(scattered, 1)
                    pool.indirect_dma_start(
                        out=acc[k], out_offset=bass.IndirectOffsetOnAxis(ap=rows[:, slot, k:k + 1], axis=0),
                        in_=merged[:, slot, k, :], in_offset=None, compute_op=ALU.add).then_inc(acc_rows[k], 16)

            def g_tile1(t, last, i, j):
                g_gather(j, 48 * REPEATS * (TILES + 1) + 32 * t + 32, y_tab, g_dst)
                g_scatter(BATON1 + t * STEPS1 + 5, acc[0], NC, j, g_uses(REPEATS, i, j))

            for par in range(2):
                pool.wait_ge(y_out[par], 80)
            with pool.If(flag > 0):
                with pool.Fori(0, PAIRS) as i:
                    for j in range(SIX):
                        scatter(i * SIX + j, j % 3)
                scatter(OCTETS - 1, 0)
                for k in range(ACCS):
                    pool.wait_ge(acc_rows[k], 16 * (OCTETS + 1))
            with pool.Else():
                for k in range(ACCS):
                    pool.wait_ge(acc_rows[k], 16)
                tiles(pool, g_tile1)
            pool.sem_inc(acc_done, 1)

        @block.tensor
        def _(pe):
            pe.wait_ge(weights, 16 * 20)
            pe.wait_ge(consts, 8)
            pe.matmul(bank[6][0:NC, 0:3 * NC], b2t[:, :], wiht[:, :], start=True, stop=True).then_inc(b2w, 1)
            pe.wait_ge(b2w, 2)

            flag = fits(pe)

            def g_merge(step, width):
                hold(pe, baton, step + 1)
                pe.transpose(bank[2][:, 0:P], g_key[:, 0:1].to_broadcast([P, P]), ident[:, :]).then_inc(baton, 1)
                hold(pe, baton, step + 3)
                pe.matmul(bank[5][:, 0:width], g_same[:, :], g_vals[:, 0:width], start=True, stop=True
                          ).then_inc(baton, 1)

            with pe.Fori(0, REPEATS) as r:
                hold(pe, table, 16 * (r + 1))

                def turn_ef(q, j, i):
                    par, ch = j % 2, j // OC % 2
                    if j % OC == 0:
                        hold(pe, ef_in[ch], 16 * (r * NCH[ch] + i + 1))
                    hold(pe, ef_copied, r * OCTETS + q + 1)
                    for b in range(2):
                        at = (j % OC * OT + 4 * b) * FD
                        mm = pe.transpose(bank[6][0:4 * FD, (2 * par + b) * P:(2 * par + b + 1) * P],
                                          ef_sb[:, ch, at:at + 4 * FD], ident[:, :])
                    mm.then_inc(ef_turned, 1)

                def hidden(q, j):
                    par = j % 2
                    hold(pe, ef_copied, HALF0 + r * OCTETS + q + 1)
                    hold(pe, h_done, r * OCTETS + q + 1)
                    pe.matmul(bank[7][:, 2 * par * P:2 * (par + 1) * P], w1bd[:, :], eft[:, par, :],
                              start=True, stop=True).then_inc(h_summed, 1)

                def edge_matrices(q, j, t):
                    hold(pe, prod_done, PROD0 + 4 * (r * OCTETS + q - 1) + t + 1)
                    for b in range(2):
                        mm = pe.matmul(bank[t][:, MW * b:MW * (b + 1)],
                                       ht[HID * t:HID * (t + 1), j % 2, P * b:P * (b + 1)],
                                       w2s[HID * t:HID * (t + 1), :], start=True, stop=True,
                                       tile_position=(HID * t, 0))
                    mm.then_inc(w_done, 1)

                def segment_sums(q, j, ck, last=False):
                    carries = (j % OC == OC - 1 or last) and not (isinstance(ck, int) and ck == 0)
                    hold(pe, hot_done, r * OCTETS + q + 1)
                    hold(pe, x_copied, XC0 + r * OCTETS + q + 1)
                    if j % OC == 0:
                        hold(pe, win_out, 2 * (r * CHUNKS + ck) + 2)
                    for t in range(4):
                        hold(pe, half_done, 4 * (r * OCTETS + q) + t + 1)
                        for b in range(2):
                            k = 4 * b + t
                            mm = pe.matmul(bank[4 + j // OC % 2][:, 0:AW], onehot[:, j % 2, k, :],
                                           terms[:, j % 2, k, :], start=(j % OC == 0 and k == 0),
                                           stop=((j % OC == OC - 1 or last) and k == OT - 1))
                        if carries and t == 2:
                            hold(pe, carry_done, r * (CHUNKS - 1) + ck)
                            hold(pe, win_out, 2 * (r * CHUNKS + ck) + 4)
                            pe.matmul(bank[4 + j // OC % 2][:, 0:GW], carry[:, j // OC % 2, :],
                                      win[:, 1 - j // OC % 2, :], start=False, stop=False)
                    mm.then_inc(octet_summed, 1)

                def octet(q, j, i, first=False, last=False):
                    if not last:
                        turn_ef(q + 1, (j + 1) % SIX, i if j < SIX - 1 else i + 1)
                    hold(pe, h_done, HALF0 + r * OCTETS + q + 1)
                    for t in range(4):
                        edge_matrices(q, j, t)
                    if not last:
                        hidden(q + 1, (j + 1) % SIX)
                    if j > 0:
                        segment_sums(q - 1, j - 1, i * 2 + (j - 1) // OC)
                    elif not first:
                        segment_sums(q - 1, SIX - 1, i * 2 - 1)

                def g_tile(t, last, i, j):
                    n = r * (TILES + 1) + t
                    step = n * STEPS0
                    hold(pe, g_in, 48 * n + 48)
                    pe.transpose(bank[6][0:FD, 0:P], g_ef[:, :], ident[:, :]).then_inc(baton, 1)
                    hold(pe, baton, step + 3)
                    pe.matmul(bank[7][0:HID, 0:P], w1bd[0:FD, 0:HID], eft[0:FD, 0, 0:P], start=True, stop=True
                              ).then_inc(baton, 1)
                    hold(pe, baton, step + 5)
                    pe.matmul(bank[0][:, 0:MW], ht[0:HID, 0, 0:P], w2s[0:HID, :], start=True, stop=True
                              ).then_inc(baton, 1)
                    g_merge(step + 6, GW)

                with pe.If(flag > 0):
                    turn_ef(0, 0, 0)
                    hidden(0, 0)
                    for j in range(SIX):
                        octet(j, j, 0, first=(j == 0))
                    with pe.Fori(1, PAIRS) as i:
                        for j in range(SIX):
                            octet(i * SIX + j, j, i)
                    octet(OCTETS - 1, 0, PAIRS, last=True)
                    segment_sums(OCTETS - 1, 0, FULL, last=True)
                with pe.Else():
                    tiles(pe, g_tile)

                hold(pe, own, own_base(r) + 3)

                def turn_gin(u, par):
                    hold(pe, gin_copied, GU * r + u + 1)
                    hold(pe, gin_staged, GU * r + u + 1)
                    for k in range(GT):
                        mm = pe.transpose(bank[par][0:3 * NC + 2, NP_ * k:NP_ * (k + 1)],
                                          gin_four[:, par, k, :], ident[0:NP_, 0:NP_])
                    mm.then_inc(gin_turned, 1)

                def gate_sums(u, par):
                    hold(pe, gin_copied, GU * r + u + 3)
                    hold(pe, gate_copied, GU * r + u + 1)
                    for k in range(GT):
                        mm = pe.matmul(bank[2 + par][0:NP_, 4 * NC * k:4 * NC * (k + 1)],
                                       gint[:, par, NP_ * k:NP_ * (k + 1)], wc[:, :], start=True, stop=True)
                    mm.then_inc(gate_summed, 1)

                turn_gin(0, 0)
                with pe.Fori(0, GU // 2) as v:
                    turn_gin(v * 2 + 1, 1)
                    gate_sums(v * 2, 0)
                    turn_gin(v * 2 + 2, 0)
                    gate_sums(v * 2 + 1, 1)
                gate_sums(GU - 1, 0)

            pe.wait_ge(x2_out, 16)

            def turn1(q, j):
                par = j % 2
                hold(pe, hot1, 3 * q + 3)
                for h in range(2):
                    hold(pe, same_done, 2 * q + h + 1)
                    for k in range(4):
                        g = 4 * h + k
                        to = bank[(2, 6)[par] + h][:, P * k:P * (k + 1)]
                        pe.matmul(to, src_hi[:, par, g:g + 1].to_broadcast([P, P]), ident_b[:, :],
                                  start=True, stop=False)
                        mm = pe.matmul(to, src_lo[:, par, g:g + 1].to_broadcast([P, P]), ident_b[:, :],
                                       start=False, stop=True)
                    mm.then_inc(turned1, 1)
                hold(pe, oht_done, q + 1)
                for k in range(OT):
                    mm = pe.transpose(bank[par][:, :].bitcast(BF16)[:, P * k:P * (k + 1)], hot[:, par, k, :],
                                      ident_b[:, :])
                mm.then_inc(turned1, 1)

            def merge1(q, par):
                hold(pe, v_copied, q + 3)
                hold(pe, same_done, 2 * q + 6)
                hold(pe, m_copied, q + 3)
                for k in range(OT):
                    mm = pe.matmul(bank[5][:, P * par + NC * k:P * par + NC * (k + 1)], same[:, par, k, :],
                                   vals[:, par, k, :], start=True, stop=True)
                mm.then_inc(m_done, 1)

            def octet1(q, j, i, first=False, last=False):
                par, ch = j % 2, j // OC % 2
                if not last:
                    turn1(q + 1, j + 1)
                if j % OC == 0:
                    hold(pe, ywin_in[ch], 16 * (i + 1))
                hold(pe, oht_done, q + 3)
                hold(pe, v_copied, q + 2)
                for k in range(OT):
                    mm = pe.matmul(bank[4][:, P * par + NC * k:P * par + NC * (k + 1)], oht[:, par, P * k:P * (k + 1)],
                                   ywin[:, ch, :], start=True, stop=True)
                mm.then_inc(v_done, 1)
                if not first:
                    merge1(q - 1, 1 - par)

            with pe.If(flag > 0):
                turn1(0, 0)
                for j in range(SIX):
                    octet1(j, j, 0, first=(j == 0))
                with pe.Fori(1, PAIRS) as i:
                    for j in range(SIX):
                        octet1(i * SIX + j, j, i)
                octet1(OCTETS - 1, 0, PAIRS, last=True)
                merge1(OCTETS - 1, 0)
            with pe.Else():
                tiles(pe, lambda t, last, i, j: g_merge(BATON1 + t * STEPS1 + 1, NC))

        @block.scalar
        def _(act):
            act.sem_inc(ef_copied, HALF0)
            act.sem_inc(h_done, HALF0)
            act.sem_inc(x_copied, XC0)
            act.sem_inc(gin_copied, 2)
            act.sem_inc(oht_done, 2)
            act.sem_inc(v_copied, 2)
            act.sem_inc(m_copied, 3)
            act.wait_ge(b2w, 1)
            act.wait_ge(wc_zero, 1)
            act.copy(wc[0:NC, 0:3 * NC], bank[6][0:NC, 0:3 * NC]).then_inc(b2w, 1)

            flag = fits(act)

            with act.Fori(0, REPEATS) as r:
                hold(act, table, 16 * (r + 1))

                def octet(q, j, i):
                    par = j % 2
                    hold(act, ef_turned, EDGE0 + r * OCTETS + q + 1)
                    hold(act, h_summed, r * OCTETS + q + 1)
                    act.copy(eft[:, par, :], bank[6][0:4 * FD, 2 * par * P:2 * (par + 1) * P]).then_inc(ef_copied, 1)
                    hold(act, h_summed, HALF0 + r * OCTETS + q + 1)
                    hold(act, w_done, W0 + 4 * (r * OCTETS + q - 1))
                    act.activation(ht[:, par, :], bank[7][:, 2 * par * P:2 * (par + 1) * P], ACT.Relu,
                                   bias=b1c[:, 0:1]).then_inc(h_done, 1)
                    hold(act, gathered[j], 128 * (r * NSLOT[j] + i + 1))
                    hold(act, octet_summed, r * OCTETS + q + 1)
                    act.copy(terms[:, par, :, 0:NC], xg[:, j, :, :]).then_inc(x_copied, 1)

                def g_tile(t, last, i, j):
                    step = (r * (TILES + 1) + t) * STEPS0
                    hold(act, baton, step + 2)
                    act.copy(eft[0:FD, 0, 0:P], bank[6][0:FD, 0:P]).then_inc(baton, 1)
                    hold(act, baton, step + 4)
                    act.activation(ht[0:HID, 0, 0:P], bank[7][0:HID, 0:P], ACT.Relu, bias=b1c[0:HID, 0:1]
                                   ).then_inc(baton, 1)

                with act.If(flag > 0):
                    with act.Fori(0, PAIRS) as i:
                        for j in range(SIX):
                            octet(i * SIX + j, j, i)
                    octet(OCTETS - 1, 0, PAIRS)
                with act.Else():
                    tiles(act, g_tile)

                def gin_copy(u, par):
                    hold(act, gin_turned, GU * r + u + 1)
                    hold(act, gate_summed, GU * r + u + 1)
                    act.copy(gint[:, par, :], bank[par][0:3 * NC + 2, 0:GT * NP_]).then_inc(gin_copied, 1)

                def gin_stage(u, par):
                    act.copy(gin_four[:, par, :, :], gin[:, bass.ds(u * GT, GT), :]).then_inc(gin_staged, 1)

                hold(act, own, own_base(r) + 3)
                gin_stage(0, 0)
                with act.Fori(0, GU // 2) as v:
                    for par in range(2):
                        gin_stage(v * 2 + par + 1, 1 - par)
                        gin_copy(v * 2 + par, par)
                gin_copy(GU - 1, 0)
                hold(act, gate_copied, GU * (r + 1) + 2)
                act.activation(gates[:, :, 0:2 * NC], gates[:, :, 0:2 * NC], ACT.Sigmoid).then_inc(act_gates, 1)
                hold(act, own, own_base(r) + 5)
                act.activation(gates[:, :, 2 * NC:3 * NC], gates[:, :, 2 * NC:3 * NC], ACT.Tanh
                               ).then_inc(act_gates, 1)

            def root(n):
                act.wait_ge(own, OWN_LN[n])
                act.activation(stat[:, 1, :], stat[:, 1, :], ACT.Sqrt).then_inc(ln_sqrt, 1)

            root(0)

            def hots_out(q, par):
                hold(act, v_done, q + 5)
                hold(act, turned1, EDGE0 + 3 * q + 3)
                act.copy(oht[:, par, :], bank[par][:, :].bitcast(BF16)).then_inc(oht_done, 1)

            def values_out(q, par):
                hold(act, v_done, q + 7)
                hold(act, m_done, q + 1)
                act.copy(vals[:, par, :, :].rearrange("p k f -> p (k f)"), bank[4][:, P * par:P * (par + 1)]
                         ).then_inc(v_copied, 1)

            def merged_out(q, par, slot):
                hold(act, m_done, q + 3)
                hold(act, scattered, q + 1)
                act.copy(merged[:, slot, :, :].rearrange("p k f -> p (k f)"), bank[5][:, P * par:P * (par + 1)]
                         ).then_inc(m_copied, 1)

            def octet1(q, j, first=False):
                if not (isinstance(q, int) and q == OCTETS - 1):
                    hots_out(q + 1, (j + 1) % 2)
                values_out(q, j % 2)
                if not first:
                    merged_out(q - 1, (j + 1) % 2, (j - 1) % 3)

            with act.If(flag > 0):
                hots_out(0, 0)
                for j in range(SIX):
                    octet1(j, j, first=(j == 0))
                with act.Fori(1, PAIRS) as i:
                    for j in range(SIX):
                        octet1(i * SIX + j, j)
                octet1(OCTETS - 1, 0)
                merged_out(OCTETS - 1, 0, 0)
            root(1)

        @block.vector
        def _(dve):
            dve.sem_inc(prod_done, PROD0)
            dve.sem_inc(agg_rows, 32)
            dve.sem_inc(win_out, 4)
            dve.sem_inc(gate_copied, 2)
            dve.sem_inc(same_done, 4)
            dve.sem_inc(rows_done, EDGE0)
            dve.sem_inc(ef_turned, EDGE0)
            dve.sem_inc(h_summed, HALF0)
            dve.sem_inc(w_done, W0)
            dve.sem_inc(octet_summed, 2)
            dve.sem_inc(gate_summed, 2)
            dve.sem_inc(v_done, EDGE0)
            dve.sem_inc(m_done, 2)
            dve.sem_inc(scattered, 2)
            dve.sem_inc(turned1, EDGE0)
            dve.sem_inc(baton, 1)

            steps = [0]

            def step(ins):
                ins.then_inc(prep, 1)
                steps[0] += 1
                return steps[0]

            dve.wait_ge(dst_in, 48)
            n = step(dve.tensor_copy(dst_rel[:, :], dst_i[:, :]))
            dve.wait_ge(prep, n)
            full = dst_rel[:, 0:FULL * G].rearrange("p (c g) -> p c g", g=G)
            tail = dst_rel[:, FULL * G:]
            step(dve.tensor_reduce(span[:, 0, 0:FULL], full, AX, ALU.max))
            step(dve.tensor_reduce(span[:, 0, FULL:], tail, AX, ALU.max))
            step(dve.tensor_reduce(span[:, 1, 0:FULL], full, AX, ALU.min))
            n = step(dve.tensor_reduce(span[:, 1, FULL:], tail, AX, ALU.min))
            dve.wait_ge(prep, n)
            n = step(dve.tensor_scalar(span[:, 1, :], span[:, 1, :], -1.0, None, ALU.mult))
            assert n == PREP_SPAN
            dve.wait_ge(spans_out, 1)
            dve.wait_ge(consts, 6)
            step(dve.tensor_scalar(base_f[:, :], spanr[:, 1, :], -1.0, None, ALU.mult))
            n = step(dve.tensor_tensor(width[:, :], spanr[:, 0, :], spanr[:, 1, :], ALU.add))
            dve.wait_ge(prep, n)
            step(dve.tensor_copy(base_i[:, :], base_f[:, :]))
            step(dve.tensor_tensor(moved[:, 1:], base_f[:, 1:], base_f[:, 0:CHUNKS - 1], ALU.subtract))
            step(dve.tensor_reduce(widest[:, :], width[:, :], AX, ALU.max))
            step(dve.tensor_tensor(full, full, base_f[:, 0:FULL].unsqueeze(2).to_broadcast([P, FULL, G]),
                                   ALU.subtract))
            n = step(dve.tensor_scalar(tail, tail, base_f[:, FULL:], None, ALU.subtract))
            assert n == PREP_REL
            dve.wait_ge(prep, n)
            n = step(dve.tensor_reduce(ordered[:, :], moved[:, 1:], AX, ALU.min))
            step(dve.tensor_scalar(carry_to[:, 1:], moved[:, 1:], -1.0, part[:, 0:1], ALU.mult, ALU.add))
            dve.wait_ge(prep, n)
            n = step(dve.tensor_scalar(ordered[:, :], ordered[:, :], 0.0, None, ALU.is_ge))
            dve.wait_ge(prep, n)
            n = step(dve.scalar_tensor_tensor(out=windowed[:, :], in0=widest[:, :], scalar=float(P),
                                              in1=ordered[:, :], op0=ALU.is_lt, op1=ALU.mult))
            assert n == PREP_FLAG
            step(dve.tensor_scalar(g_valid[:, :], part[:, 0:1], float(TDUP), None, ALU.is_ge))
            step(dve.memset(g_vals[:, NC:NC + 1], 1.0))
            dve.wait_ge(consts, 8)
            step(dve.tensor_copy(ident_b[:, :], ident[:, :]))
            step(dve.memset(terms[:, :, :, NC:NC + 1], 1.0))
            n = step(dve.memset(gin[:, :, 3 * NC:], 1.0))
            step(dve.tensor_copy(gin[:, :, 2 * NC:3 * NC], xs[:, :, :]))
            dve.wait_ge(masked, 1)
            dve.wait_ge(prep, n + 1)

            flag = fits(dve)

            def g_after(ins, count):
                ins.then_inc(g_own, 1)
                hold(dve, g_own, count)

            def g_keys(step, own_at, index, last):
                if last:
                    g_after(dve.tensor_copy(g_away[:, :], index[:, :]), own_at + 1)
                    g_after(dve.tensor_tensor(g_away[:, :], g_away[:, :], dummy[:, :], ALU.subtract), own_at + 2)
                    dve.scalar_tensor_tensor(out=g_key[:, :], in0=g_away[:, :], scalar=g_valid[:, 0:1],
                                             in1=dummy[:, :], op0=ALU.mult, op1=ALU.add).then_inc(baton, 1)
                else:
                    dve.tensor_copy(g_key[:, :], index[:, :]).then_inc(baton, 1)

            def g_rows_of(step, own_at, width):
                hold(dve, baton, step + 1)
                dve.tensor_scalar(g_same[:, :], bank[2][:, 0:P], g_key[:, 0:1], None, ALU.is_equal).then_inc(baton, 1)
                hold(dve, baton, step + 3)
                g_after(dve.tensor_tensor(g_early[:, :], g_same[:, :], before[:, :], ALU.mult), own_at + 1)
                g_after(dve.tensor_reduce(g_count[:, :], g_early[:, :], AX, ALU.max), own_at + 2)
                g_after(dve.tensor_tensor(g_away[:, :], dummy[:, :], g_key[:, :], ALU.subtract), own_at + 3)
                g_after(dve.scalar_tensor_tensor(out=g_rows[:, :], in0=g_away[:, :], scalar=g_count[:, 0:1],
                                                 in1=g_key[:, :], op0=ALU.mult, op1=ALU.add), own_at + 4)
                dve.tensor_copy(g_sum[:, 0:width], bank[5][:, 0:width]).then_inc(baton, 1)

            with dve.Fori(0, REPEATS) as r:
                hold(dve, table, 16 * (r + 1))
                B = own_base(r)

                def after(ins, k):
                    ins.then_inc(own, 1)
                    dve.wait_ge(own, own_base(r) + k)

                def window_out(ck, par):
                    hold(dve, octet_summed, 2 + r * OCTETS + minimum(ck))
                    hold(dve, agg_rows, 16 * (r * CHUNKS + ck + 1))
                    dve.tensor_copy(win[:, par, 0:NC + 1], bank[4 + par][:, 0:NC + 1]).then_inc(win_out, 1)
                    dve.tensor_reduce(win[:, par, NC + 1:], bank[4 + par][:, NC + 1:AW].rearrange(
                        "p (i o) -> p o i", o=NC), AX, ALU.add).then_inc(win_out, 1)

                def carry_hots(ck, par):
                    dve.tensor_scalar(carry[:, par, :], cols[:, :], carry_to[:, bass.ds(ck, 1)], None, ALU.is_equal
                                      ).then_inc(carry_done, 1)

                def minimum(ck):
                    return ck * OC + OC if not isinstance(ck, int) or ck < FULL else OCTETS

                def hots(q, par, last_sum):
                    dve.tensor_tensor(onehot[:, par, :, :], cols[:, :].unsqueeze(1).to_broadcast([P, OT, P]),
                                      dst_rel[:, bass.ds(q * OT, OT)].unsqueeze(2).to_broadcast([P, OT, P]),
                                      ALU.is_equal).then_inc(hot_done, 1)

                def halve(q, par, t):
                    hold(dve, prod_done, PROD0 + 4 * (r * OCTETS + q) + t + 1)
                    dve.tensor_tensor(terms[:, par, t::4, NC + 1:], prod[:, t, :, 0:HW], prod[:, t, :, HW:MW],
                                      ALU.add).then_inc(half_done, 1)

                def octet(q, j, i, out_of=None):
                    par = j % 2
                    hold(dve, octet_summed, r * OCTETS + q + 1)
                    hots(q, par, None)
                    hold(dve, gathered[j], 128 * (r * NSLOT[j] + i + 1))
                    for t in range(4):
                        hold(dve, w_done, W0 + 4 * (r * OCTETS + q) + t + 1)
                        dve.tensor_tensor(
                            prod[:, t, :, :].rearrange("p b (i o) -> p b i o", i=NC),
                            bank[t][:, :].rearrange("p (b i o) -> p b i o", b=2, i=NC),
                            xg[:, j, t::4, :].unsqueeze(3).to_broadcast([P, 2, NC, NC]),
                            ALU.mult).then_inc(prod_done, 1)
                        if t == 1 and out_of is not None:
                            window_out(*out_of)
                            carry_hots(out_of[0] + 1, 1 - out_of[1])
                        if t >= 1:
                            halve(q, par, t - 1)
                    halve(q, par, 3)

                def turn(i, first=False):
                    for j in range(SIX):
                        out_of = None
                        if j == 1 and not first:
                            out_of = (i * 2 - 1, 1)
                        if j == OC + 1:
                            out_of = (i * 2, 0)
                        octet(i * SIX + j, j, i, out_of)

                def g_tile(t, last, i, j):
                    n = r * (TILES + 1) + t
                    step, own_at = n * STEPS0, n * 5 + r * 2
                    hold(dve, g_gathered[j], 16 * g_uses(r, i, j))
                    hold(dve, baton, step + 6)
                    g_after(dve.tensor_tensor(
                        g_prod[:, :].rearrange("p (i o) -> p i o", i=NC),
                        bank[0][:, 0:MW].rearrange("p (i o) -> p i o", i=NC),
                        g_x[:, :].unsqueeze(2).to_broadcast([P, NC, NC]), ALU.mult), own_at + 1)
                    dve.tensor_reduce(g_vals[:, NC + 1:], g_prod[:, :].rearrange("p (i o) -> p o i", i=NC), AX, ALU.add)
                    dve.tensor_copy(g_vals[:, 0:NC], g_x[:, :])
                    g_keys(step, own_at + 1, g_dst, last)
                    g_rows_of(step + 7, own_at + (3 if last else 1), GW)

                with dve.If(flag > 0):
                    turn(0, first=True)
                    with dve.Fori(1, PAIRS) as i:
                        turn(i)
                    octet(OCTETS - 1, 0, PAIRS)
                    window_out(FULL - 1, 1)
                    carry_hots(FULL, 0)
                    window_out(FULL, 0)
                with dve.Else():
                    tiles(dve, g_tile)

                hold(dve, agg_in, 16 * (r + 1))
                after(dve.tensor_scalar(inv[:, :], aggl[:, :, NC:NC + 1].rearrange("p j a -> p (j a)"), 1.0, None,
                                        ALU.max), 1)
                dve.reciprocal(inv[:, :], inv[:, :]).then_inc(own, 1)
                hold(dve, own, own_base(r) + 2)
                spread = inv[:, :].unsqueeze(2).to_broadcast([NP_, NJ, NC])
                dve.tensor_tensor(gin[:, :, 0:NC], aggl[:, :, 0:NC], spread, ALU.mult)
                dve.tensor_tensor(gin[:, :, NC:2 * NC], aggl[:, :, NC + 1:], spread, ALU.mult).then_inc(own, 1)

                def gate_out(u, par):
                    hold(dve, gate_summed, GU * r + u + 3)
                    dve.tensor_copy(gates[:, bass.ds(u * GT, GT), :],
                                    bank[2 + par][0:NP_, 0:GT * 4 * NC].rearrange("p (k f) -> p k f", k=GT)
                                    ).then_inc(gate_copied, 1)

                with dve.Fori(0, GU // 2) as v:
                    for par in range(2):
                        gate_out(v * 2 + par, par)
                gate_out(GU - 1, 0)
                hold(dve, act_gates, 2 * r + 1)
                g_r, g_z, g_n, g_h = (gates[:, :, NC * k:NC * (k + 1)] for k in range(4))
                h = gin[:, :, 2 * NC:3 * NC]
                after(dve.tensor_tensor(g_h, g_h, g_r, ALU.mult), 4)
                dve.tensor_tensor(g_n, g_n, g_h, ALU.add).then_inc(own, 1)
                hold(dve, act_gates, 2 * r + 2)
                after(dve.tensor_tensor(g_r, h, g_n, ALU.subtract), 6)
                after(dve.tensor_tensor(g_r, g_r, g_z, ALU.mult), 7)
                after(dve.tensor_tensor(h, g_n, g_r, ALU.add), 8)

            done = [own_base(REPEATS)]

            def link(ins):
                ins.then_inc(own, 1)
                done[0] += 1
                dve.wait_ge(own, done[0])

            def layernorm(n):
                mean, var, tmp = stat[:, 0, :], stat[:, 1, :], stat[:, 2, :]
                wide = lambda v: v.unsqueeze(2).to_broadcast([NP_, NJ, NC])
                link(dve.tensor_reduce(tmp, xs[:, :, :], AX, ALU.add))
                link(dve.tensor_scalar(mean, tmp, 1.0 / NC, None, ALU.mult))
                link(dve.tensor_tensor(xs[:, :, :], xs[:, :, :], wide(mean), ALU.subtract))
                link(dve.tensor_tensor(gates[:, :, 0:NC], xs[:, :, :], xs[:, :, :], ALU.mult))
                link(dve.tensor_reduce(tmp, gates[:, :, 0:NC], AX, ALU.add))
                link(dve.tensor_scalar(var, tmp, 1.0 / NC, EPS, ALU.mult, ALU.add))
                assert done[0] == OWN_LN[n]
                dve.wait_ge(ln_sqrt, n + 1)
                link(dve.reciprocal(tmp, var))
                return dve.tensor_tensor(xs[:, :, :], xs[:, :, :], wide(tmp), ALU.mult)

            link(dve.tensor_tensor(xs[:, :, :], xs[:, :, :], gin[:, :, 2 * NC:3 * NC], ALU.add))
            link(layernorm(0))
            assert done[0] == OWN_X2

            dve.wait_ge(table, 16 * (REPEATS + 1))

            def hots1(q, j, i):
                par, ch = j % 2, j // OC % 2
                if j % OC == 0:
                    hold(dve, s1_in[ch], 16 * (i + 1))
                hold(dve, turned1, 3 * q + 3)
                dve.tensor_tensor(hot[:, par, :, :], cols[:, :].unsqueeze(1).to_broadcast([P, OT, P]),
                                  dst_rel[:, bass.ds(q * OT, OT)].unsqueeze(2).to_broadcast([P, OT, P]),
                                  ALU.is_equal).then_inc(hot1, 1)
                hold(dve, rows_done, q + 5)
                g = j % OC * OT
                dve.tensor_copy(srcf[:, par, :], src_i[:, ch, g:g + OT]).then_inc(own_hot, 1)
                dve.tensor_scalar(src_low[:, par, :], src_i[:, ch, g:g + OT], P - 1, None, ALU.bitwise_and
                                  ).then_inc(own_hot, 1)
                hold(dve, own_hot, 2 * q + 2)
                dve.tensor_copy(src_lo[:, par, :], src_low[:, par, :]).then_inc(hot1, 1)
                dve.tensor_tensor(src_hi[:, par, :], srcf[:, par, :], src_low[:, par, :], ALU.subtract
                                  ).then_inc(hot1, 1)

            def octet1(q, j, i, slot, last=False):
                par, ch = j % 2, j // OC % 2
                if not last:
                    hots1(q + 1, (j + 1) % SIX, i if j < SIX - 1 else i + 1)
                hold(dve, m_done, q + 1)
                dve.tensor_scalar(away[:, :], srcf[:, par, :], -1.0, dummy[:, 0:1], ALU.mult, ALU.add
                                  ).then_inc(own1, 1)
                for h in range(2):
                    hold(dve, turned1, EDGE0 + 3 * q + h + 1)
                    dve.tensor_tensor(
                        same[:, par, 4 * h:4 * h + 4, :],
                        bank[(2, 6)[par] + h][:, :].rearrange("p (k e) -> p k e", k=4),
                        srcf[:, par, 4 * h:4 * h + 4].unsqueeze(2).to_broadcast([P, 4, P]), ALU.is_equal
                    ).then_inc(same_done, 1)
                hold(dve, same_done, 2 * q + 6)
                dve.tensor_tensor(earlier[:, :, :], same[:, par, :, :],
                                  before[:, :].unsqueeze(1).to_broadcast([P, OT, P]), ALU.mult).then_inc(own1, 1)
                hold(dve, own1, 4 * q + 2)
                dve.tensor_reduce(count[:, :], earlier[:, :, :], AX, ALU.max).then_inc(own1, 1)
                hold(dve, own1, 4 * q + 3)
                dve.tensor_tensor(shift[:, :], count[:, :], away[:, :], ALU.mult).then_inc(own1, 1)
                hold(dve, own1, 4 * q + 4)
                hold(dve, scattered, q + 1)
                dve.tensor_tensor(rows[:, slot, :], srcf[:, par, :], shift[:, :], ALU.add).then_inc(rows_done, 1)

            def g_tile1(t, last, i, j):
                step, own_at = BATON1 + t * STEPS1, REPEATS * (5 * (TILES + 1) + 2) + 4 * t
                hold(dve, g_gathered[j], 16 * g_uses(REPEATS, i, j))
                dve.tensor_copy(g_vals[:, 0:NC], g_x[:, :])
                g_keys(step, own_at, g_src, last)
                g_rows_of(step + 2, own_at + (2 if last else 0), NC)

            with dve.If(flag > 0):
                hots1(0, 0, 0)
                with dve.Fori(0, PAIRS) as i:
                    for j in range(SIX):
                        octet1(i * SIX + j, j, i, j % 3)
                octet1(OCTETS - 1, 0, PAIRS, 0, last=True)
            with dve.Else():
                tiles(dve, g_tile1)

            for half in range(2):
                dve.wait_ge(acc_in, 64 * (half + 1))
                for k in range(4):
                    link(dve.tensor_tensor(xs[:, :, :], xs[:, :, :], gates[:, :, NC * k:NC * (k + 1)], ALU.add))
                if half == 0:
                    dve.sem_inc(acc_used, 1)
            layernorm(1).then_inc(result, 1)


PREP_SPAN, PREP_REL, PREP_FLAG = 6, 13, 17


def own_base(r):
    return r * 8


OWN_X2 = own_base(REPEATS) + 9
OWN_LN = [own_base(REPEATS) + 7, OWN_X2 + 8 + 6]
STEPS0, STEPS1 = 11, 6
BATON1 = REPEATS * (TILES + 1) * STEPS0

_INS = ['x', 'src', 'dst', 'edge_attr_13', 'L0_gnn_fnet_w1', 'L0_gnn_fnet_b1', 'L0_gnn_fnet_w2', 'L0_gnn_fnet_b2',
        'L0_gnn_gru_w_ih', 'L0_gnn_gru_w_hh', 'L0_gnn_gru_b_ih', 'L0_gnn_gru_b_hh']


def kernel(**inputs):
    import numpy as np
    import concourse.bacc as bacc
    from concourse import mybir
    from concourse.bass_utils import run_bass_kernel_spmd

    nc = bacc.Bacc("TRN2", target_bir_lowering=False, num_devices=1)
    arrays, args = {}, []
    for name in _INS:
        a = np.ascontiguousarray(inputs[name])
        arrays[f"in_{name}"] = a
        args.append(nc.dram_tensor(f"in_{name}", a.shape, mybir.dt.from_np(a.dtype), kind="ExternalInput").ap())
    args.append(nc.dram_tensor("out_0", (NODES, NC), mybir.dt.float32, kind="ExternalOutput").ap())
    program(nc, *args)
    run = run_bass_kernel_spmd(nc, [arrays], core_ids=[0])
    return run.results[0]["out_0"]
```

```python
from contextlib import ExitStack

import concourse.bass as bass
from concourse import mybir
from concourse.alu_op_type import AluOpType as ALU

F32 = mybir.dt.float32
I32 = mybir.dt.int32
BF16 = mybir.dt.bfloat16
ACT = mybir.ActivationFunctionType
AX = mybir.AxisListType.X

P = 128
NODES, NC = 12500, 16
EDGES, FD = 412500, 13
HID = 32
REPEATS = 2
OT = 8
G = 24
OC = G // OT
CE = P * G
FULL = EDGES // CE
CHUNKS = FULL + 1
TE = P * OT
PAIRS = FULL // 2
SIX = 2 * OC
OCTETS = FULL * OC + 1
DUP = TE - (EDGES - FULL * CE)
assert FULL % 2 == 0 and 0 <= DUP and G % OT == 0
NP_, NJ = 125, 100
ROWS = 99 * P
MW = NC * NC
HW = MW // 2
AW = NC + 1 + HW
GW = 2 * NC + 1
GT = 4
GU = NJ // GT
ACCS = 8
DT = (2, 1)
ST = OT - min(DT)
MODS = P // NC
SB = 4
CW = -(-NODES // (MODS * SB * 8)) * 8
DW = SB * CW
BLOCKS, BREST = DW // P, DW % P
KW = 64
assert GU % 2 and KW == 4 * NC
YCHUNKS = -(-NODES // CE)
YOCTETS = YCHUNKS * OC
EPS = 1e-5
TILES = EDGES // P
TDUP = P - EDGES % P
TURN = 6
assert EDGES % P and TDUP > 0 and TILES % TURN == 0

PROD0, XC0, HALF0, W0, EDGE0 = 4 * SIX, SIX, 2, 8, SIX


def program(nc, x, src, dst, ef, w1, b1, w2, b2, wih, whh, bih, bhh, out):
    with ExitStack() as ctx:
        def sb(name, shape, dt=F32):
            return ctx.enter_context(nc.sbuf_tensor(name, shape, dt))

        def sem(name):
            return ctx.enter_context(nc.semaphore(name))

        def hold(eng, s, value):
            eng.wait_ge(s, value)
            eng.nop(nofuse=True)

        hx_tab = nc.dram_tensor("hx_tab", [NODES, NC], F32).ap()
        agg = nc.dram_tensor("agg", [ROWS, GW], F32).ap()
        x2_tab = nc.dram_tensor("x2_tab", [ROWS, NC], F32).ap()
        y_tab = nc.dram_tensor("y_tab", [YCHUNKS * CE, NC], F32).ap()
        acc = [nc.dram_tensor(f"acc{k}", [ROWS, NC], F32).ap() for k in range(ACCS)]

        ident = sb("ident", [P, P])
        before = sb("before", [P, P])
        before_b = sb("before_b", [P, P], BF16)
        cols = sb("col_no", [P, P])
        part = sb("part_no", [P, 1])
        dummy = sb("spare", [P, 1])
        zeros = sb("zeros", [P, ROWS * GW // P])
        w1bd = sb("w1bd", [4 * FD, 4 * HID])
        b1c = sb("b1c", [P, 1])
        w2s = sb("w2s", [P, MW])
        wc = sb("wc", [P, 2 * 4 * NC])
        b2t = sb("b2t", [NC, NC])
        wiht = sb("wiht", [NC, 3 * NC])

        dst_i = sb("dst_i", [P, OCTETS * OT], I32)
        dst_rel = sb("dst_rel", [P, OCTETS * OT])
        span = sb("span", [P, 2, CHUNKS])
        spanr = sb("spanr", [P, 2, CHUNKS])
        width = sb("width", [P, CHUNKS])
        base_f = sb("base_f", [P, CHUNKS])
        base_i = sb("base_i", [P, CHUNKS], I32)
        moved = sb("moved", [P, CHUNKS])
        carry_to = sb("carry_to", [P, CHUNKS])
        ordered = sb("ordered", [P, 1])
        widest = sb("widest", [P, 1])
        windowed = sb("windowed", [P, 1], I32)

        src_i = sb("src_i", [P, 2, G], I32)
        ef_sb = sb("ef_sb", [P, 2, G * FD])
        eft = sb("eft", [4 * FD, 2, 2 * P])
        ht = sb("ht", [P, 2, 2 * P])
        xg = sb("xg", [P, SIX, OT, NC])
        onehot = sb("onehot", [P, 2, OT, P])
        prod = sb("prod", [P, 4, 2, MW])
        terms = sb("terms", [P, 2, OT, AW])
        win = sb("win", [P, 2, GW])
        carry = sb("carry", [P, 2, P])

        xs = sb("xs", [NP_, NJ, NC])
        aggl = sb("aggl", [NP_, NJ, GW])
        gin = sb("gin", [NP_, NJ, KW])
        gin_four = sb("gin_four", [NP_, 2, GT, KW])
        gint = sb("gint", [P, 2, GT // 2 * NP_])
        h_new = sb("h_new", [NP_, NJ, NC])
        gates = sb("gates", [NP_, NJ, 4 * NC])
        inv = sb("inv", [NP_, NJ])
        stat = sb("stat", [NP_, 3, NJ])

        yidx = sb("yidx", [NP_, 2, 10], I32)
        yg = sb("yg", [NP_, 2, 10, NC])
        ywin = sb("ywin", [P, 2, NC])
        ywin_parts = sb("ywin_parts", [P, 2, 3, NC], BF16)
        rest = sb("rest", [P, NC])
        hot = sb("hot", [P, 2, OT, P], BF16)
        srcf = sb("srcf", [P, 2, OT])
        src_low = sb("src_low", [P, 2, OT], I32)
        src_lo = sb("src_lo", [P, 2, OT], BF16)
        src_hi = sb("src_hi", [P, 2, OT], BF16)
        ident_b = sb("ident_b", [P, P], BF16)
        oht = sb("oht", [P, 2, OT * P], BF16)
        same = sb("same", [P, 2, ST, P], BF16)
        earlier = sb("earlier", [P, ST, P], BF16)
        count = sb("count", [P, ST])
        away = sb("away", [P, ST])
        shift = sb("shift", [P, ST])
        vals = sb("vals", [P, 2, OT, NC])
        val_parts = sb("val_parts", [P, 2, OT, 3, NC], BF16)
        merged = sb("merged", [P, 3, ST, NC])
        rows = sb("rows", [P, 3, ST], I32)
        eights = sb("eights", [P, DW])
        one = sb("one", [P, 1])
        src_mod = sb("src_mod", [P, 3, 2], I32)
        src_neg = sb("src_neg", [P, 3, 2])
        mod_hot = sb("mod_hot", [P, 3, 2, MODS], BF16)
        placed = sb("placed", [P, sum(DT), 3, P], BF16)
        div_hot = dst_i[:, :].bitcast(BF16)[:, 0:sum(DT) * DW].rearrange("p (a e) -> p a e", a=sum(DT))
        off = terms[:, :, :, :].rearrange("p a k f -> p (a k f)").bitcast(BF16)[:, 0:2 * DW].rearrange(
            "p (a e) -> p a e", a=2)
        tot = onehot[:, :, :, :].rearrange("p a k e -> p (a k e)")[:, 0:DW]
        tot_rows = prod[:, :, :, :].rearrange("p t b m -> p (t b m)")[:, 0:(BLOCKS + 1) * P]

        bank = [ctx.enter_context(nc.psum_tensor(f"bank{k}", [P, 512], F32)) for k in range(8)]

        g_src = sb("g_src", [P, 1], I32)
        g_dst = sb("g_dst", [P, 1], I32)
        g_ef = sb("g_ef", [P, FD])
        g_x = sb("g_x", [P, NC])
        g_prod = sb("g_prod", [P, MW])
        g_vals = sb("g_vals", [P, GW])
        g_key = sb("g_key", [P, 1])
        g_valid = sb("g_valid", [P, 1])
        g_same = sb("g_same", [P, P])
        g_early = sb("g_early", [P, P])
        g_count = sb("g_count", [P, 1])
        g_away = sb("g_away", [P, 1])
        g_rows = sb("g_rows", [P, 1], I32)
        g_sum = sb("g_sum", [P, GW])

        consts = sem("consts")
        weights = sem("weights")
        w1_zero = sem("w1_zero")
        wc_zero = sem("wc_zero")
        dst_in = sem("dst_in")
        prep = sem("prep")
        spans_out = sem("spans_out")
        masked = sem("masked")
        b2w = sem("b2w")
        table = sem("table")
        src_in = [sem(f"src_in{k}") for k in range(2)]
        ef_in = [sem(f"ef_in{k}") for k in range(2)]
        ef_turned = sem("ef_turned")
        ef_copied = sem("ef_copied")
        h_summed = sem("h_summed")
        h_done = sem("h_done")
        w_done = sem("w_done")
        gathered = [sem(f"gathered{k}") for k in range(SIX)]
        prod_done = sem("prod_done")
        half_done = sem("half_done")
        x_copied = sem("x_copied")
        hot_done = sem("hot_done")
        octet_summed = sem("octet_summed")
        win_out = sem("win_out")
        carry_done = sem("carry_done")
        agg_zero = sem("agg_zero")
        agg_rows = sem("agg_rows")
        agg_in = sem("agg_in")
        gin_done = sem("gin_done")
        gin_staged = sem("gin_staged")
        gin_turned = sem("gin_turned")
        gin_copied = sem("gin_copied")
        gate_summed = sem("gate_summed")
        gate_copied = sem("gate_copied")
        act_gates = sem("act_gates")
        own = sem("own")
        own1 = sem("own1")
        own_hot = sem("own_hot")
        x2_out = sem("x2_out")
        ln_sqrt = sem("ln_sqrt")
        x2_zero = sem("x2_zero")
        yidx_in = [sem(f"yidx_in{k}") for k in range(2)]
        y_in = [sem(f"y_in{k}") for k in range(2)]
        y_out = [sem(f"y_out{k}") for k in range(2)]
        y_hot, y_turned, y_oht = sem("y_hot"), sem("y_turned"), sem("y_oht")
        y_val, y_copied = sem("y_val"), sem("y_copied")
        y_stored = [sem(f"y_stored{k}") for k in range(2)]
        y_win = [sem(f"y_win{k}") for k in range(2)]
        y_ready = sem("y_ready")
        acc_zero = sem("acc_zero")
        h_saved = sem("h_saved")
        ywin_in = [sem(f"ywin_in{k}") for k in range(2)]
        s1_in = [sem(f"s1_in{k}") for k in range(2)]
        hot1 = sem("hot1")
        turned1 = sem("turned1")
        oht_done = sem("oht_done")
        same_done = sem("same_done")
        rows_done = sem("rows_done")
        v_done = sem("v_done")
        v_copied = sem("v_copied")
        m_done = sem("m_done")
        m_copied = sem("m_copied")
        own_split = sem("own_split")
        split_done = sem("split_done")
        div_ready = sem("div_ready")
        own_div = sem("own_div")
        div_done = sem("div_done")
        placed_done = sem("placed_done")
        direct_done = sem("direct_done")
        tot_copied, tot_turned, tot_out = sem("tot_copied"), sem("tot_turned"), sem("tot_out")
        tot_stored = sem("tot_stored")
        acc_rows = [sem(f"acc_rows{k}") for k in range(ST)]
        scattered = sem("scattered")
        acc_in = [sem(f"acc_in{k}") for k in range(ACCS)]
        result = sem("result")
        out_done = sem("out_done")

        sums_done = sem("sums_done")
        acc_done = sem("acc_done")
        baton = sem("baton")
        g_in = sem("g_in")
        g_gathered = [sem(f"g_gathered{j}") for j in range(TURN)]
        g_landed = [sem(f"g_landed{j}") for j in range(TURN)]
        g_own = sem("g_own")

        block = ctx.enter_context(nc.Block())

        def direct_tiles(par):
            return [(OT - DT[par] + d, d, par * DT[0] + d) for d in range(DT[par])]

        def scattered_tiles(par):
            return OT - DT[par]

        def direct_before(q, j, i):
            pair = (q // 2) if isinstance(q, int) else i * (SIX // 2) + j // 2
            return pair * sum(DT) + j % 2 * DT[0]

        def fits(eng):
            eng.wait_ge(prep, PREP_FLAG)
            return eng.value_load(windowed[0:1, 0:1], min_val=0, max_val=1)

        def tiles(eng, tile):
            with eng.Fori(0, TILES // TURN) as i:
                for j in range(TURN):
                    tile(i * TURN + j, False, i, j)
            tile(TILES, True, TILES // TURN, 0)

        def g_uses(run, i, j):
            return run * (TILES // TURN + (j == 0)) + i + 1

        NSLOT = [PAIRS + 1] + [PAIRS] * (SIX - 1)
        NCH = [PAIRS + 1, PAIRS]
        SRC_FULL = src[0:FULL * CE].rearrange("(c p g) -> c p g", p=P, g=G)
        EF_FULL = ef[0:FULL * CE, :].rearrange("(c p g) f -> c p (g f)", p=P, g=G)
        SRC_TAIL = src[EDGES - TE:EDGES].rearrange("(p g) -> p g", g=OT)
        EF_TAIL = ef[EDGES - TE:EDGES, :].rearrange("(p g) f -> p (g f)", g=OT)

        def loaded_table(k):
            buffer = gates if k < 4 else gin
            return buffer[:, :, :].rearrange("p j f -> p (j f)")[:, NJ * NC * (k % 4):NJ * NC * (k % 4 + 1)]

        @block.sync
        def _(sp):
            def src_load(c, par, ring_in):
                if c is None:
                    sp.dma_start(src_i[:, par, 0:OT], SRC_TAIL).then_inc(ring_in[par], 16)
                else:
                    sp.dma_start(src_i[:, par, :], SRC_FULL[bass.ds(c, 1), :, :].rearrange("a p g -> (a p) g")
                                 ).then_inc(ring_in[par], 16)

            sp.dma_start(dst_i[:, 0:FULL * G].rearrange("p (c g) -> p c g", g=G),
                         dst[0:FULL * CE].rearrange("(c p g) -> p c g", p=P, g=G)).then_inc(dst_in, 16)
            sp.dma_start(dst_i[:, FULL * G:], dst[EDGES - TE:EDGES].rearrange("(p g) -> p g", g=OT)
                         ).then_inc(dst_in, 16)
            sp.dma_start(hx_tab, x).then_inc(table, 16)
            sp.dma_start(xs[:, :, :], x.rearrange("(p j) f -> p j f", j=NJ)).then_inc(dst_in, 16)
            sp.wait_ge(w1_zero, 1)
            for k in range(4):
                sp.dma_start(w1bd[FD * k:FD * (k + 1), HID * k:HID * (k + 1)], w1).then_inc(weights, 16)
                sp.dma_start(b1c[HID * k:HID * (k + 1), :], b1.rearrange("(k a) -> k a", a=1)).then_inc(weights, 16)
                sp.dma_start(w2s[HID * k:HID * (k + 1), :], w2).then_inc(weights, 16)
            sp.wait_ge(wc_zero, 1)

            def row(v):
                return v.rearrange("(a k) -> a k", a=1)

            with nc.allow_non_contiguous_dma(reason="768 weights, once"):
                sp.dma_start(wiht[:, :], wih.rearrange("o i -> i o")).then_inc(weights, 16)
                sp.dma_start(b2t[:, :], b2.rearrange("(i o) -> o i", o=NC)).then_inc(weights, 16)
                for k in range(2):
                    w = wc[KW * k:KW * (k + 1), 4 * NC * k:4 * NC * (k + 1)]
                    sp.dma_start(w[NC:2 * NC, 0:3 * NC], wih.rearrange("o i -> i o")).then_inc(weights, 16)
                    sp.dma_start(w[2 * NC:3 * NC, 0:2 * NC], whh[0:2 * NC, :].rearrange("o i -> i o")
                                 ).then_inc(weights, 16)
                    sp.dma_start(w[2 * NC:3 * NC, 3 * NC:4 * NC], whh[2 * NC:3 * NC, :].rearrange("o i -> i o")
                                 ).then_inc(weights, 16)
                    sp.dma_start(w[3 * NC:3 * NC + 1, 0:3 * NC], row(bih)).then_inc(weights, 16)
                    sp.dma_start(w[3 * NC + 1:3 * NC + 2, 0:2 * NC], row(bhh[0:2 * NC])).then_inc(weights, 16)
                    sp.dma_start(w[3 * NC + 1:3 * NC + 2, 3 * NC:4 * NC], row(bhh[2 * NC:3 * NC])).then_inc(weights, 16)
            sp.wait_ge(consts, 1)

            sp.dma_start(x2_tab[NODES:ROWS, :].rearrange("(p r) f -> p (r f)", p=86), zeros[0:86, 0:2 * NC]
                         ).then_inc(x2_zero, 16)

            flag = fits(sp)

            def g_load(first_step, t, last, attributes):
                hold(sp, baton, first_step + 1)
                e = EDGES - P if last else t * P
                sp.dma_start(g_src[:, :], src[bass.ds(e, P)].rearrange("(p a) -> p a", a=1)).then_inc(g_in, 16)
                sp.dma_start(g_dst[:, :], dst[bass.ds(e, P)].rearrange("(p a) -> p a", a=1)).then_inc(g_in, 16)
                if attributes:
                    sp.dma_start(g_ef[:, :], ef[bass.ds(e, P), :]).then_inc(g_in, 16)

            with sp.Fori(0, REPEATS) as r:
                def zero():
                    sp.dma_start(agg.rearrange("(p r) f -> p (r f)", p=P), zeros[:, :]).then_inc(agg_zero, 16)
                    for k in range(ACCS):
                        sp.dma_start(acc[k].rearrange("(p r) f -> p (r f)", p=P), zeros[:, 0:ROWS * NC // P]
                                     ).then_inc(acc_zero, 16)

                def load0(c, par, ck):
                    hold(sp, ef_turned, EDGE0 + r * OCTETS + (ck - 1) * OC)
                    if c is None:
                        sp.dma_start(ef_sb[:, par, 0:OT * FD], EF_TAIL).then_inc(ef_in[par], 16)
                    else:
                        sp.dma_start(ef_sb[:, par, :], EF_FULL[bass.ds(c, 1), :, :].rearrange("a p g -> (a p) g")
                                     ).then_inc(ef_in[par], 16)
                    hold(sp, prod_done, PROD0 + (r * OCTETS + (ck - 1) * OC) * 4)
                    src_load(c, par, src_in)

                def store_window(c, par):
                    hold(sp, win_out, 4 + 2 * (r * CHUNKS + c) + 2)
                    hold(sp, agg_rows, 16 * (r * CHUNKS + c + 2))
                    first = sp.value_load(base_i[0:1, bass.ds(c, 1)], min_val=0, max_val=NODES - 1)
                    sp.dma_start(agg[bass.ds(first, P), :], win[:, par, :]).then_inc(agg_rows, 16)

                with sp.If(flag > 0):
                    for par in range(2):
                        load0(par, par, par)
                    zero()
                    hold(sp, agg_zero, 16 * (r + 1))
                    with sp.Fori(1, PAIRS) as i:
                        for par in range(2):
                            load0(i * 2 + par, par, i * 2 + par)
                            store_window(i * 2 + par - 2, par)
                    load0(None, 0, FULL)
                    store_window(FULL - 2, 0)
                    store_window(FULL - 1, 1)
                    store_window(FULL, 0)
                    hold(sp, agg_rows, 16 * (r + 1) * CHUNKS + 32)
                with sp.Else():
                    zero()
                    tiles(sp, lambda t, last, i, j: g_load((r * (TILES + 1) + t) * STEPS0, t, last, True))
                    hold(sp, sums_done, r + 1)
                sp.dma_start(aggl[:, :, :], agg[0:NODES, :].rearrange("(p j) f -> p j f", j=NJ)).then_inc(agg_in, 16)
                hold(sp, own, own_base(r + 1))
                sp.dma_start(hx_tab.rearrange("(p j) f -> p j f", j=NJ), h_new[:, :, :]).then_inc(table, 16)
            hold(sp, own, OWN_X2)
            sp.dma_start(x2_tab[0:NODES, :].rearrange("(p j) f -> p j f", j=NJ), xs[:, :, :]).then_inc(x2_out, 16)

            def y_general():
                YI = dst[0:NODES].rearrange("(p b k) -> b p k", p=NP_, k=10)
                YO = y_tab[0:NODES, :].rearrange("(p b k) f -> b p (k f)", p=NP_, k=10)
                for par in range(2):
                    sp.dma_start(yidx[:, par, :], YI[par]).then_inc(yidx_in[par], 16)

                def y_store(i, last=False):
                    for par in range(2):
                        hold(sp, y_in[par], 160 * (i + 1))
                        sp.dma_start(YO[bass.ds(i * 2 + par, 1), :, :].rearrange("a p k -> (a p) k"),
                                     yg[:, par, :, :].rearrange("p k f -> p (k f)")).then_inc(y_out[par], 16)
                        if not last:
                            sp.dma_start(yidx[:, par, :], YI[bass.ds(i * 2 + par + 2, 1), :, :].rearrange(
                                "a p k -> (a p) k")).then_inc(yidx_in[par], 16)

                with sp.Fori(0, 4) as i:
                    y_store(i)
                y_store(4, last=True)
                for par in range(2):
                    hold(sp, y_out[par], 80)

            def y_windows():
                hold(sp, x2_out, 16)
                hold(sp, x2_zero, 16)

                def window(c):
                    first = sp.value_load(base_i[0:1, c:c + 1], min_val=0, max_val=NODES - 1)
                    sp.dma_start(ywin[:, c % 2, :], x2_tab[bass.ds(first, P), :]).then_inc(y_win[c % 2], 16)

                window(0)
                window(1)
                rows = y_tab.rearrange("(c p g) f -> c p (g f)", p=P, g=G)
                for q in range(YOCTETS):
                    c, o = q // OC, q % OC
                    hold(sp, y_copied, 2 + q + 1)
                    sp.dma_start(rows[c, :, P * o:P * (o + 1)], vals[:, q % 2, :, :].rearrange("p k f -> p (k f)")
                                 ).then_inc(y_stored[q % 2], 16)
                    if o == OC - 1 and c + 2 < YCHUNKS:
                        window(c + 2)
                for par in range(2):
                    hold(sp, y_stored[par], 16 + 16 * ((YOCTETS + 1 - par) // 2))

            with sp.If(flag > 0):
                y_windows()
            with sp.Else():
                y_general()
            sp.sem_inc(y_ready, 1)

            def load1(c, par, ck):
                hold(sp, rows_done, EDGE0 + (ck - 1) * OC)
                src_load(c, par, s1_in)
                hold(sp, v_done, EDGE0 + (ck - 1) * OC)
                first = sp.value_load(base_i[0:1, bass.ds(ck, 1)], min_val=0, max_val=NODES - 1)
                sp.dma_start(ywin[:, par, :], y_tab[bass.ds(first, P), :]).then_inc(ywin_in[par], 16)

            with sp.If(flag > 0):
                with sp.Fori(0, PAIRS) as i:
                    for par in range(2):
                        load1(i * 2 + par, par, i * 2 + par)
                load1(None, 0, FULL)
                hold(sp, acc_zero, 16 * ACCS * REPEATS)
                hold(sp, tot_out, SB)
                full = BLOCKS * P * MODS
                sp.dma_start(acc[ACCS - 1][0:full, :].rearrange("(b p m) f -> p b (m f)", p=P, m=MODS),
                             tot_rows[:, 0:BLOCKS * P].rearrange("p (b x) -> p b x", x=P)).then_inc(tot_stored, 16)
                sp.dma_start(acc[ACCS - 1][full:full + BREST * MODS, :].rearrange("(p m) f -> p (m f)", m=MODS),
                             tot_rows[0:BREST, BLOCKS * P:]).then_inc(tot_stored, 16)
                hold(sp, tot_stored, 32)
            with sp.Else():
                tiles(sp, lambda t, last, i, j: g_load(BATON1 + t * STEPS1, t, last, False))
            hold(sp, acc_done, 1)
            for k in range(ACCS):
                sp.dma_start(loaded_table(k), acc[k][0:NODES, :].rearrange("(p j) f -> p (j f)", j=NJ)
                             ).then_inc(acc_in[k], 16)
            hold(sp, result, 1)
            sp.dma_start(out.rearrange("(p j) f -> p j f", j=NJ), xs[:, :, :]).then_inc(out_done, 16)
            hold(sp, out_done, 16)
            hold(sp, table, 16 * (REPEATS + 1))
            hold(sp, x2_out, 16)
            hold(sp, x2_zero, 16)

        @block.gpsimd
        def _(pool):
            pool.memset(w1bd[:, :], 0.0).then_inc(w1_zero, 1)
            pool.memset(wc[:, :], 0.0).then_inc(wc_zero, 1)
            pool.memset(zeros[:, :], 0.0).then_inc(consts, 1)
            pool.memset(ident[:, :], 1.0).then_inc(consts, 1)
            pool.memset(before[:, :], 1.0).then_inc(consts, 1)
            pool.iota(cols[:, :], [[1, P]], base=0, channel_multiplier=0,
                      allow_small_or_imprecise_dtypes=True).then_inc(consts, 1)
            pool.iota(part[:, :], [[0, 1]], base=0, channel_multiplier=1,
                      allow_small_or_imprecise_dtypes=True).then_inc(consts, 1)
            pool.iota(dummy[:, :], [[0, 1]], base=NODES, channel_multiplier=1,
                      allow_small_or_imprecise_dtypes=True).then_inc(consts, 1)
            pool.wait_ge(consts, 6)
            pool.affine_select(out=ident[:, :], in_=ident[:, :], pattern=[[-1, P]], compare_op=ALU.is_equal,
                               fill=0.0, base=0, channel_multiplier=1).then_inc(consts, 1)
            pool.affine_select(out=before[:, :], in_=before[:, :], pattern=[[-1, P]], compare_op=ALU.is_gt,
                               fill=0.0, base=0, channel_multiplier=1).then_inc(consts, 1)
            pool.wait_ge(prep, PREP_SPAN)
            pool.partition_all_reduce(spanr[:, :, :].rearrange("p a c -> p (a c)"),
                                      span[:, :, :].rearrange("p a c -> p (a c)"), P,
                                      bass.bass_isa.ReduceOp.max).then_inc(spans_out, 1)
            pool.wait_ge(prep, PREP_REL)
            tail = dst_rel[:, FULL * G:]
            pool.affine_select(out=tail, in_=tail, pattern=[[1, OT]], compare_op=ALU.is_ge, fill=-1.0,
                               base=-DUP, channel_multiplier=OT).then_inc(masked, 1)
            pool.memset(one[:, :], 1.0).then_inc(consts, 1)
            pool.iota(eights[:, :], [[MODS, DW]], base=0, channel_multiplier=0,
                      allow_small_or_imprecise_dtypes=True).then_inc(consts, 1)

            flag = fits(pool)

            def g_gather(j, at, tab, index):
                hold(pool, g_in, at)
                pool.indirect_dma_start(
                    out=g_x[:, :], out_offset=None, in_=tab,
                    in_offset=bass.IndirectOffsetOnAxis(ap=index[:, :], axis=0)).then_inc(g_gathered[j], 16)

            def g_scatter(step, tab, width, j, uses):
                hold(pool, baton, step + 1)
                pool.indirect_dma_start(
                    out=tab, out_offset=bass.IndirectOffsetOnAxis(ap=g_rows[:, :], axis=0),
                    in_=g_sum[:, 0:width], in_offset=None, compute_op=ALU.add).then_inc(g_landed[j], 16)
                hold(pool, g_landed[j], 16 * uses)
                pool.sem_inc(baton, 1)

            with pool.Fori(0, REPEATS) as r:
                hold(pool, table, 16 * (r + 1))

                def gather(q, j, i):
                    if j % OC == 0:
                        hold(pool, src_in[j // OC % 2], 16 * (r * NCH[j // OC % 2] + i + 1))
                    hold(pool, prod_done, 4 * (r * OCTETS + q) + 4)
                    hold(pool, x_copied, r * OCTETS + q + 1)
                    for k in range(OT):
                        g = j % OC * OT + k
                        pool.indirect_dma_start(
                            out=xg[:, j, k, :], out_offset=None, in_=hx_tab,
                            in_offset=bass.IndirectOffsetOnAxis(ap=src_i[:, j // OC, g:g + 1], axis=0)
                        ).then_inc(gathered[j], 16)

                def g_tile(t, last, i, j):
                    n = r * (TILES + 1) + t
                    g_gather(j, 48 * n + 48, hx_tab, g_src)
                    g_scatter(n * STEPS0 + 10, agg, GW, j, g_uses(r, i, j))

                with pool.If(flag > 0):
                    with pool.Fori(0, PAIRS) as i:
                        for j in range(SIX):
                            gather(i * SIX + j, j, i)
                    gather(OCTETS - 1, 0, PAIRS)
                with pool.Else():
                    hold(pool, agg_zero, 16 * (r + 1))
                    tiles(pool, g_tile)
                    pool.sem_inc(sums_done, 1)

            def y_gather(i, first=False):
                for par in range(2):
                    hold(pool, yidx_in[par], 16 * (i + 1))
                    if not first:
                        hold(pool, y_out[par], 16 * i)
                    for k in range(10):
                        pool.indirect_dma_start(
                            out=yg[:, par, k, :], out_offset=None, in_=x2_tab,
                            in_offset=bass.IndirectOffsetOnAxis(ap=yidx[:, par, k:k + 1], axis=0)
                        ).then_inc(y_in[par], 16)

            def scatter(q, j, first=False):
                hold(pool, m_copied, q + 4)
                hold(pool, rows_done, EDGE0 + q + 1)
                tiles = scattered_tiles(j % 2)
                for k in range(tiles):
                    if k == ST - 1 and not (isinstance(q, int) and q == 1):
                        hold(pool, acc_rows[k], 8 * (q - 1))
                    elif k < ST - 1 and not first:
                        hold(pool, acc_rows[k], 16 * q)
                    if k == tiles - 1:
                        if tiles < ST and not first:
                            hold(pool, acc_rows[ST - 1], 8 * q)
                        pool.sem_inc(scattered, 1)
                    pool.indirect_dma_start(
                        out=acc[k], out_offset=bass.IndirectOffsetOnAxis(ap=rows[:, j % 3, k:k + 1], axis=0),
                        in_=merged[:, j % 3, k, :], in_offset=None, compute_op=ALU.add).then_inc(acc_rows[k], 16)

            def g_tile1(t, last, i, j):
                g_gather(j, 48 * REPEATS * (TILES + 1) + 32 * t + 32, y_tab[0:NODES, :], g_dst)
                g_scatter(BATON1 + t * STEPS1 + 5, acc[0], NC, j, g_uses(REPEATS, i, j))

            pool.wait_ge(x2_out, 16)
            pool.wait_ge(acc_zero, 16 * ACCS * REPEATS)
            with pool.If(flag > 0):
                for j in range(SIX):
                    scatter(j, j, first=(j == 0))
                with pool.Fori(1, PAIRS) as i:
                    for j in range(SIX):
                        scatter(i * SIX + j, j)
                scatter(OCTETS - 1, 0)
                for k in range(ST):
                    pool.wait_ge(acc_rows[k], 16 * (OCTETS if k < ST - 1 else OCTETS // 2))
            with pool.Else():
                y_gather(0, first=True)
                with pool.Fori(1, 5) as i:
                    y_gather(i)
                pool.wait_ge(y_ready, 1)
                tiles(pool, g_tile1)
            pool.sem_inc(acc_done, 1)

        @block.tensor
        def _(pe):
            pe.wait_ge(weights, 16 * 26)
            pe.wait_ge(consts, 8)
            pe.matmul(bank[6][0:NC, 0:3 * NC], b2t[:, :], wiht[:, :], start=True, stop=True).then_inc(b2w, 1)
            pe.wait_ge(b2w, 3)

            flag = fits(pe)

            def g_merge(step, width):
                hold(pe, baton, step + 1)
                pe.transpose(bank[2][:, 0:P], g_key[:, 0:1].to_broadcast([P, P]), ident[:, :]).then_inc(baton, 1)
                hold(pe, baton, step + 3)
                pe.matmul(bank[5][:, 0:width], g_same[:, :], g_vals[:, 0:width], start=True, stop=True
                          ).then_inc(baton, 1)

            with pe.Fori(0, REPEATS) as r:
                hold(pe, table, 16 * (r + 1))

                def turn_ef(q, j, i):
                    par, ch = j % 2, j // OC % 2
                    if j % OC == 0:
                        hold(pe, ef_in[ch], 16 * (r * NCH[ch] + i + 1))
                    hold(pe, ef_copied, r * OCTETS + q + 1)
                    for b in range(2):
                        at = (j % OC * OT + 4 * b) * FD
                        mm = pe.transpose(bank[6][0:4 * FD, (2 * par + b) * P:(2 * par + b + 1) * P],
                                          ef_sb[:, ch, at:at + 4 * FD], ident[:, :])
                    mm.then_inc(ef_turned, 1)

                def hidden(q, j):
                    par = j % 2
                    hold(pe, ef_copied, HALF0 + r * OCTETS + q + 1)
                    hold(pe, h_done, r * OCTETS + q + 1)
                    pe.matmul(bank[7][:, 2 * par * P:2 * (par + 1) * P], w1bd[:, :], eft[:, par, :],
                              start=True, stop=True).then_inc(h_summed, 1)

                def edge_matrices(q, j, t):
                    hold(pe, prod_done, PROD0 + 4 * (r * OCTETS + q - 1) + t + 1)
                    for b in range(2):
                        mm = pe.matmul(bank[t][:, MW * b:MW * (b + 1)],
                                       ht[HID * t:HID * (t + 1), j % 2, P * b:P * (b + 1)],
                                       w2s[HID * t:HID * (t + 1), :], start=True, stop=True,
                                       tile_position=(HID * t, 0))
                    mm.then_inc(w_done, 1)

                def segment_sums(q, j, ck, last=False):
                    carries = (j % OC == OC - 1 or last) and not (isinstance(ck, int) and ck == 0)
                    hold(pe, hot_done, r * OCTETS + q + 1)
                    hold(pe, x_copied, XC0 + r * OCTETS + q + 1)
                    if j % OC == 0:
                        hold(pe, win_out, 2 * (r * CHUNKS + ck) + 2)
                    for t in range(4):
                        hold(pe, half_done, 4 * (r * OCTETS + q) + t + 1)
                        for b in range(2):
                            k = 4 * b + t
                            mm = pe.matmul(bank[4 + j // OC % 2][:, 0:AW], onehot[:, j % 2, k, :],
                                           terms[:, j % 2, k, :], start=(j % OC == 0 and k == 0),
                                           stop=((j % OC == OC - 1 or last) and k == OT - 1))
                        if carries and t == 2:
                            hold(pe, carry_done, r * (CHUNKS - 1) + ck)
                            hold(pe, win_out, 2 * (r * CHUNKS + ck) + 4)
                            pe.matmul(bank[4 + j // OC % 2][:, 0:GW], carry[:, j // OC % 2, :],
                                      win[:, 1 - j // OC % 2, :], start=False, stop=False)
                    mm.then_inc(octet_summed, 1)

                def octet(q, j, i, first=False, last=False):
                    if not last:
                        turn_ef(q + 1, (j + 1) % SIX, i if j < SIX - 1 else i + 1)
                    hold(pe, h_done, HALF0 + r * OCTETS + q + 1)
                    for t in range(4):
                        edge_matrices(q, j, t)
                    if not last:
                        hidden(q + 1, (j + 1) % SIX)
                    if j > 0:
                        segment_sums(q - 1, j - 1, i * 2 + (j - 1) // OC)
                    elif not first:
                        segment_sums(q - 1, SIX - 1, i * 2 - 1)

                def g_tile(t, last, i, j):
                    n = r * (TILES + 1) + t
                    step = n * STEPS0
                    hold(pe, g_in, 48 * n + 48)
                    pe.transpose(bank[6][0:FD, 0:P], g_ef[:, :], ident[:, :]).then_inc(baton, 1)
                    hold(pe, baton, step + 3)
                    pe.matmul(bank[7][0:HID, 0:P], w1bd[0:FD, 0:HID], eft[0:FD, 0, 0:P], start=True, stop=True
                              ).then_inc(baton, 1)
                    hold(pe, baton, step + 5)
                    pe.matmul(bank[0][:, 0:MW], ht[0:HID, 0, 0:P], w2s[0:HID, :], start=True, stop=True
                              ).then_inc(baton, 1)
                    g_merge(step + 6, GW)

                with pe.If(flag > 0):
                    turn_ef(0, 0, 0)
                    hidden(0, 0)
                    for j in range(SIX):
                        octet(j, j, 0, first=(j == 0))
                    with pe.Fori(1, PAIRS) as i:
                        for j in range(SIX):
                            octet(i * SIX + j, j, i)
                    octet(OCTETS - 1, 0, PAIRS, last=True)
                    segment_sums(OCTETS - 1, 0, FULL, last=True)
                with pe.Else():
                    tiles(pe, g_tile)

                hold(pe, own, own_base(r) + 3)

                def turn_gin(u, par):
                    hold(pe, gin_copied, GU * r + u + 1)
                    hold(pe, gin_staged, GU * r + u + 1)
                    for k in range(GT // 2):
                        mm = pe.transpose(bank[par][:, NP_ * k:NP_ * (k + 1)],
                                          gin_four[:, par, 2 * k:2 * k + 2, :].rearrange("p k f -> p (k f)"),
                                          ident[0:NP_, 0:NP_])
                    mm.then_inc(gin_turned, 1)

                def gate_sums(u, par):
                    hold(pe, gin_copied, GU * r + u + 3)
                    hold(pe, gate_copied, GU * r + u + 1)
                    for k in range(GT // 2):
                        mm = pe.matmul(bank[2 + par][0:NP_, 8 * NC * k:8 * NC * (k + 1)],
                                       gint[:, par, NP_ * k:NP_ * (k + 1)], wc[:, :], start=True, stop=True)
                    mm.then_inc(gate_summed, 1)

                turn_gin(0, 0)
                with pe.Fori(0, GU // 2) as v:
                    turn_gin(v * 2 + 1, 1)
                    gate_sums(v * 2, 0)
                    turn_gin(v * 2 + 2, 0)
                    gate_sums(v * 2 + 1, 1)
                gate_sums(GU - 1, 0)


            def y_turn(q, par):
                hold(pe, y_hot, q + 1)
                hold(pe, y_oht, q + 1)
                for k in range(OT):
                    mm = pe.transpose(bank[par][:, :].bitcast(BF16)[:, P * k:P * (k + 1)], hot[:, par, k, :],
                                      ident_b[:, :])
                mm.then_inc(y_turned, 1)

            def y_rows(q, j, last=False):
                par, ch = j % 2, j // OC % 2
                if not last:
                    y_turn(q + 1, 1 - par)
                if j % OC == 0:
                    hold(pe, split_done, q // OC + 2)
                hold(pe, y_oht, q + 3)
                hold(pe, y_copied, q + 1)
                for k in range(OT):
                    for n in range(3):
                        mm = pe.matmul(bank[4 + par][:, NC * k:NC * (k + 1)], oht[:, par, P * k:P * (k + 1)],
                                       ywin_parts[:, ch, n, :], start=(n == 0), stop=(n == 2))
                mm.then_inc(y_val, 1)

            def turn1(q, j):
                par = j % 2
                hold(pe, hot1, 3 * q + 3)
                for h in range(2):
                    hold(pe, same_done, 2 * q + h + 3)
                    for g in range(4 * h, min(4 * h + 4, scattered_tiles(par))):
                        to = bank[6 + h][:, P * (g - 4 * h):P * (g - 4 * h + 1)]
                        pe.matmul(to, src_hi[:, par, g:g + 1].to_broadcast([P, P]), ident_b[:, :],
                                  start=True, stop=False)
                        mm = pe.matmul(to, src_lo[:, par, g:g + 1].to_broadcast([P, P]), ident_b[:, :],
                                       start=False, stop=True)
                    mm.then_inc(turned1, 1)
                hold(pe, oht_done, q + 2)
                for k in range(OT):
                    mm = pe.transpose(bank[4][:, :].bitcast(BF16)[:, P * k:P * (k + 1)], hot[:, par, k, :],
                                      ident_b[:, :])
                mm.then_inc(turned1, 1)

            def merge1(q, par):
                hold(pe, v_copied, q + 3)
                hold(pe, same_done, 2 * q + 6)
                for k in range(scattered_tiles(par)):
                    for n in range(3):
                        mm = pe.matmul(bank[5][:, NC * k:NC * (k + 1)], same[:, par, k, :],
                                       val_parts[:, par, k, n, :], start=(n == 0), stop=(n == 2))
                mm.then_inc(m_done, 1)

            def direct(q, j, i, which, first=False, last=False):
                if which >= DT[j % 2]:
                    return
                k, d, slot = direct_tiles(j % 2)[which]
                hold(pe, placed_done, q + 4)
                hold(pe, div_done, direct_before(q, j, i) + d + 4)
                for n in range(3):
                    for b in range(SB):
                        mm = pe.matmul(bank[b][:, 0:CW], placed[:, slot, n, :], div_hot[:, slot, CW * b:CW * (b + 1)],
                                       start=(first and d == 0 and n == 0), stop=(last and k == OT - 1 and n == 2))
                mm.then_inc(direct_done, 1)

            def values(q, j, i):
                if j % OC == 0:
                    hold(pe, split_done, YCHUNKS + i * 2 + j // OC + 2)
                hold(pe, oht_done, q + 3)
                hold(pe, m_copied, q + 3)
                for k in range(OT):
                    mm = pe.matmul(bank[5][:, 3 * NC * k:3 * NC * (k + 1)], oht[:, j % 2, P * k:P * (k + 1)],
                                   ywin_parts[:, j // OC % 2, :, :].rearrange("p n f -> p (n f)"),
                                   start=True, stop=True)
                mm.then_inc(v_done, 1)

            def octet1(q, j, i, first=False, start=False, last=False):
                if not last:
                    turn1(q + 1, j + 1)
                merge1(q, j % 2)
                before = (q - 1, j - 1, i) if j > 0 else (q - 1, SIX - 1, i - 1)
                if not first:
                    direct(*before, 0, first=start)
                if not last:
                    values(q + 1, (j + 1) % SIX, i if j < SIX - 1 else i + 1)
                if not first:
                    direct(*before, 1)

            with pe.If(flag > 0):
                y_turn(0, 0)
                for q in range(YOCTETS):
                    y_rows(q, q % SIX, last=(q == YOCTETS - 1))
                turn1(0, 0)
                values(0, 0, 0)
                for j in range(SIX):
                    octet1(j, j, 0, first=(j == 0), start=(j == 1))
                with pe.Fori(1, PAIRS) as i:
                    for j in range(SIX):
                        octet1(i * SIX + j, j, i)
                octet1(OCTETS - 1, 0, PAIRS, last=True)
                for which in range(DT[0]):
                    direct(OCTETS - 1, 0, PAIRS, which, last=True)
                hold(pe, oht_done, OCTETS + 2)
                hold(pe, same_done, 2 * OCTETS + 4)
                hold(pe, m_copied, OCTETS + 3)
                hold(pe, tot_copied, SB)
                for b in range(BLOCKS + 1):
                    width = P if b < BLOCKS else BREST
                    mm = pe.transpose(bank[4 + b // 4][0:width, P * (b % 4):P * (b % 4 + 1)],
                                      tot[:, P * b:P * b + width], ident[:, :])
                    if b % 4 == 3 or b == BLOCKS:
                        mm.then_inc(tot_turned, 1)
            with pe.Else():
                tiles(pe, lambda t, last, i, j: g_merge(BATON1 + t * STEPS1 + 1, NC))

        @block.scalar
        def _(act):
            act.sem_inc(ef_copied, HALF0)
            act.sem_inc(h_done, HALF0)
            act.sem_inc(x_copied, XC0)
            act.sem_inc(gin_copied, 2)
            act.sem_inc(y_oht, 2)
            act.sem_inc(oht_done, 2)
            act.sem_inc(div_done, 3)
            act.sem_inc(v_copied, 2)
            act.sem_inc(m_copied, 3)
            act.wait_ge(b2w, 1)
            act.wait_ge(wc_zero, 1)
            for k in range(2):
                act.copy(wc[KW * k:KW * k + NC, 4 * NC * k:4 * NC * k + 3 * NC], bank[6][0:NC, 0:3 * NC]
                         ).then_inc(b2w, 1)

            flag = fits(act)

            with act.Fori(0, REPEATS) as r:
                hold(act, table, 16 * (r + 1))

                def octet(q, j, i):
                    par = j % 2
                    hold(act, ef_turned, EDGE0 + r * OCTETS + q + 1)
                    hold(act, h_summed, r * OCTETS + q + 1)
                    act.copy(eft[:, par, :], bank[6][0:4 * FD, 2 * par * P:2 * (par + 1) * P]).then_inc(ef_copied, 1)
                    hold(act, h_summed, HALF0 + r * OCTETS + q + 1)
                    hold(act, w_done, W0 + 4 * (r * OCTETS + q - 1))
                    act.activation(ht[:, par, :], bank[7][:, 2 * par * P:2 * (par + 1) * P], ACT.Relu,
                                   bias=b1c[:, 0:1]).then_inc(h_done, 1)
                    hold(act, gathered[j], 128 * (r * NSLOT[j] + i + 1))
                    hold(act, octet_summed, r * OCTETS + q + 1)
                    act.copy(terms[:, par, :, 0:NC], xg[:, j, :, :]).then_inc(x_copied, 1)

                def g_tile(t, last, i, j):
                    step = (r * (TILES + 1) + t) * STEPS0
                    hold(act, baton, step + 2)
                    act.copy(eft[0:FD, 0, 0:P], bank[6][0:FD, 0:P]).then_inc(baton, 1)
                    hold(act, baton, step + 4)
                    act.activation(ht[0:HID, 0, 0:P], bank[7][0:HID, 0:P], ACT.Relu, bias=b1c[0:HID, 0:1]
                                   ).then_inc(baton, 1)

                with act.If(flag > 0):
                    with act.Fori(0, PAIRS) as i:
                        for j in range(SIX):
                            octet(i * SIX + j, j, i)
                    octet(OCTETS - 1, 0, PAIRS)
                with act.Else():
                    tiles(act, g_tile)

                def gin_copy(u, par):
                    hold(act, gin_turned, GU * r + u + 1)
                    hold(act, gate_summed, GU * r + u + 1)
                    act.copy(gint[:, par, :], bank[par][:, 0:GT // 2 * NP_]).then_inc(gin_copied, 1)

                def gin_stage(u, par):
                    act.copy(gin_four[:, par, :, :], gin[:, bass.ds(u * GT, GT), :]).then_inc(gin_staged, 1)

                hold(act, own, own_base(r) + 3)
                gin_stage(0, 0)
                gin_stage(1, 1)
                with act.Fori(0, GU // 2 - 1) as v:
                    for par in range(2):
                        gin_copy(v * 2 + par, par)
                        gin_stage(v * 2 + par + 2, par)
                gin_copy(GU - 3, 0)
                gin_stage(GU - 1, 0)
                gin_copy(GU - 2, 1)
                gin_copy(GU - 1, 0)
                hold(act, gate_copied, GU * (r + 1) + 2)
                act.activation(gates[:, :, 0:2 * NC], gates[:, :, 0:2 * NC], ACT.Sigmoid).then_inc(act_gates, 1)
                hold(act, own, own_base(r) + 5)
                act.activation(gates[:, :, 2 * NC:3 * NC], gates[:, :, 2 * NC:3 * NC], ACT.Tanh
                               ).then_inc(act_gates, 1)
                hold(act, own, own_base(r) + 8)
                act.copy(gin[:, :, 2 * NC:3 * NC], h_new[:, :, :]).then_inc(h_saved, 1)

            def root(n):
                act.wait_ge(own, OWN_LN[n])
                act.activation(stat[:, 1, :], stat[:, 1, :], ACT.Sqrt).then_inc(ln_sqrt, 1)

            root(0)

            def y_hots_out(q, par):
                hold(act, y_val, q + 1)
                hold(act, y_turned, q + 3)
                act.copy(oht[:, par, :], bank[par][:, :].bitcast(BF16)).then_inc(y_oht, 1)

            def hots_out(q, par):
                hold(act, v_done, q + 5)
                hold(act, turned1, EDGE0 + 3 * q + 3)
                act.copy(oht[:, par, :], bank[4][:, :].bitcast(BF16)).then_inc(oht_done, 1)

            def values_out(q, par):
                hold(act, v_done, q + 7)
                hold(act, m_done, q + 1)
                hold(act, placed_done, q + 2)
                act.copy(val_parts[:, par, :, :, :].rearrange("p k n f -> p (k n f)"), bank[5][:, 0:3 * P]
                         ).then_inc(v_copied, 1)

            def merged_out(q, j):
                hold(act, m_done, q + 3)
                hold(act, scattered, q + 1)
                tiles = scattered_tiles(j % 2)
                act.copy(merged[:, j % 3, 0:tiles, :].rearrange("p k f -> p (k f)"), bank[5][:, 0:tiles * NC]
                         ).then_inc(m_copied, 1)

            def distance(q, j, i, d):
                n = direct_before(q, j, i) + d
                hold(act, div_ready, q + 1)
                hold(act, div_done, n + 3)
                act.activation(off[:, d, :], eights[:, :], ACT.Square, bias=src_neg[:, j % 3, d:d + 1]
                               ).then_inc(own_div, 1)

            def div_hots(q, j, i, d):
                n = direct_before(q, j, i) + d
                hold(act, own_div, n + 1)
                hold(act, direct_done, n + 1)
                act.activation(div_hot[:, direct_tiles(j % 2)[d][2], :], off[:, d, :], ACT.Relu, bias=one[:, 0:1],
                               scale=-1.0).then_inc(div_done, 1)

            def octet1(q, j, i):
                last = isinstance(q, int) and q == OCTETS - 1
                if not last:
                    hots_out(q + 1, (j + 1) % 2)
                if j % 2:
                    div_hots(q - 1, j - 1, i, 1)
                merged_out(q, j)
                distance(q, j, i, 0)
                if not last:
                    values_out(q + 1, (j + 1) % 2)
                div_hots(q, j, i, 0)
                if j % 2 == 0:
                    distance(q, j, i, 1)

            with act.If(flag > 0):
                for q in range(YOCTETS):
                    y_hots_out(q, q % 2)
                act.wait_ge(consts, 10)
                hots_out(0, 0)
                values_out(0, 0)
                with act.Fori(0, PAIRS) as i:
                    for j in range(SIX):
                        octet1(i * SIX + j, j, i)
                octet1(OCTETS - 1, 0, PAIRS)
                div_hots(OCTETS - 1, 0, PAIRS, 1)
                hold(act, direct_done, 3 + direct_before(OCTETS, 1, PAIRS))
                for b in range(SB):
                    act.copy(tot[:, CW * b:CW * (b + 1)], bank[b][:, 0:CW]).then_inc(tot_copied, 1)
            root(1)

        @block.vector
        def _(dve):
            dve.sem_inc(prod_done, PROD0)
            dve.sem_inc(agg_rows, 32)
            dve.sem_inc(win_out, 4)
            dve.sem_inc(gate_copied, 2)
            dve.sem_inc(same_done, 4)
            dve.sem_inc(rows_done, EDGE0)
            dve.sem_inc(ef_turned, EDGE0)
            dve.sem_inc(h_summed, HALF0)
            dve.sem_inc(w_done, W0)
            dve.sem_inc(octet_summed, 2)
            dve.sem_inc(gate_summed, 2)
            dve.sem_inc(v_done, EDGE0)
            dve.sem_inc(m_done, 2)
            dve.sem_inc(placed_done, 3)
            dve.sem_inc(split_done, 1)
            dve.sem_inc(direct_done, 3)
            dve.sem_inc(scattered, 2)
            dve.sem_inc(turned1, EDGE0)
            dve.sem_inc(y_turned, 2)
            dve.sem_inc(y_val, 2)
            dve.sem_inc(y_copied, 2)
            for k in range(2):
                dve.sem_inc(y_stored[k], 16)
            dve.sem_inc(baton, 1)

            steps = [0]

            def step(ins):
                ins.then_inc(prep, 1)
                steps[0] += 1
                return steps[0]

            dve.wait_ge(dst_in, 48)
            n = step(dve.tensor_copy(dst_rel[:, :], dst_i[:, :]))
            dve.wait_ge(prep, n)
            full = dst_rel[:, 0:FULL * G].rearrange("p (c g) -> p c g", g=G)
            tail = dst_rel[:, FULL * G:]
            step(dve.tensor_reduce(span[:, 0, 0:FULL], full, AX, ALU.max))
            step(dve.tensor_reduce(span[:, 0, FULL:], tail, AX, ALU.max))
            step(dve.tensor_reduce(span[:, 1, 0:FULL], full, AX, ALU.min))
            n = step(dve.tensor_reduce(span[:, 1, FULL:], tail, AX, ALU.min))
            dve.wait_ge(prep, n)
            n = step(dve.tensor_scalar(span[:, 1, :], span[:, 1, :], -1.0, None, ALU.mult))
            assert n == PREP_SPAN
            dve.wait_ge(spans_out, 1)
            dve.wait_ge(consts, 6)
            step(dve.tensor_scalar(base_f[:, :], spanr[:, 1, :], -1.0, None, ALU.mult))
            n = step(dve.tensor_tensor(width[:, :], spanr[:, 0, :], spanr[:, 1, :], ALU.add))
            dve.wait_ge(prep, n)
            step(dve.tensor_copy(base_i[:, :], base_f[:, :]))
            step(dve.tensor_tensor(moved[:, 1:], base_f[:, 1:], base_f[:, 0:CHUNKS - 1], ALU.subtract))
            step(dve.tensor_reduce(widest[:, :], width[:, :], AX, ALU.max))
            step(dve.tensor_tensor(full, full, base_f[:, 0:FULL].unsqueeze(2).to_broadcast([P, FULL, G]),
                                   ALU.subtract))
            n = step(dve.tensor_scalar(tail, tail, base_f[:, FULL:], None, ALU.subtract))
            assert n == PREP_REL
            dve.wait_ge(prep, n)
            n = step(dve.tensor_reduce(ordered[:, :], moved[:, 1:], AX, ALU.min))
            step(dve.tensor_scalar(carry_to[:, 1:], moved[:, 1:], -1.0, part[:, 0:1], ALU.mult, ALU.add))
            dve.wait_ge(prep, n)
            n = step(dve.tensor_scalar(ordered[:, :], ordered[:, :], 0.0, None, ALU.is_ge))
            dve.wait_ge(prep, n)
            n = step(dve.scalar_tensor_tensor(out=windowed[:, :], in0=widest[:, :], scalar=float(P),
                                              in1=ordered[:, :], op0=ALU.is_lt, op1=ALU.mult))
            assert n == PREP_FLAG
            step(dve.tensor_scalar(g_valid[:, :], part[:, 0:1], float(TDUP), None, ALU.is_ge))
            step(dve.memset(g_vals[:, NC:NC + 1], 1.0))
            dve.wait_ge(consts, 8)
            step(dve.tensor_copy(ident_b[:, :], ident[:, :]))
            step(dve.tensor_copy(before_b[:, :], before[:, :]))
            step(dve.memset(terms[:, :, :, NC:NC + 1], 1.0))
            step(dve.memset(gin[:, :, 3 * NC + 2:], 0.0))
            n = step(dve.memset(gin[:, :, 3 * NC:3 * NC + 2], 1.0))
            step(dve.tensor_copy(gin[:, :, 2 * NC:3 * NC], xs[:, :, :]))
            dve.wait_ge(masked, 1)
            dve.wait_ge(prep, steps[0])

            flag = fits(dve)

            def g_after(ins, count):
                ins.then_inc(g_own, 1)
                hold(dve, g_own, count)

            def g_keys(step, own_at, index, last):
                if last:
                    g_after(dve.tensor_copy(g_away[:, :], index[:, :]), own_at + 1)
                    g_after(dve.tensor_tensor(g_away[:, :], g_away[:, :], dummy[:, :], ALU.subtract), own_at + 2)
                    dve.scalar_tensor_tensor(out=g_key[:, :], in0=g_away[:, :], scalar=g_valid[:, 0:1],
                                             in1=dummy[:, :], op0=ALU.mult, op1=ALU.add).then_inc(baton, 1)
                else:
                    dve.tensor_copy(g_key[:, :], index[:, :]).then_inc(baton, 1)

            def g_rows_of(step, own_at, width):
                hold(dve, baton, step + 1)
                dve.tensor_scalar(g_same[:, :], bank[2][:, 0:P], g_key[:, 0:1], None, ALU.is_equal).then_inc(baton, 1)
                hold(dve, baton, step + 3)
                g_after(dve.tensor_tensor(g_early[:, :], g_same[:, :], before[:, :], ALU.mult), own_at + 1)
                g_after(dve.tensor_reduce(g_count[:, :], g_early[:, :], AX, ALU.max), own_at + 2)
                g_after(dve.tensor_tensor(g_away[:, :], dummy[:, :], g_key[:, :], ALU.subtract), own_at + 3)
                g_after(dve.scalar_tensor_tensor(out=g_rows[:, :], in0=g_away[:, :], scalar=g_count[:, 0:1],
                                                 in1=g_key[:, :], op0=ALU.mult, op1=ALU.add), own_at + 4)
                dve.tensor_copy(g_sum[:, 0:width], bank[5][:, 0:width]).then_inc(baton, 1)

            with dve.Fori(0, REPEATS) as r:
                hold(dve, table, 16 * (r + 1))

                def after(ins, k):
                    ins.then_inc(own, 1)
                    dve.wait_ge(own, own_base(r) + k)

                def window_out(ck, par):
                    hold(dve, octet_summed, 2 + r * OCTETS + octets_to(ck))
                    hold(dve, agg_rows, 16 * (r * CHUNKS + ck + 1))
                    dve.tensor_copy(win[:, par, 0:NC + 1], bank[4 + par][:, 0:NC + 1]).then_inc(win_out, 1)
                    dve.tensor_reduce(win[:, par, NC + 1:], bank[4 + par][:, NC + 1:AW].rearrange(
                        "p (i o) -> p o i", o=NC), AX, ALU.add).then_inc(win_out, 1)

                def carry_hots(ck, par):
                    dve.tensor_scalar(carry[:, par, :], cols[:, :], carry_to[:, bass.ds(ck, 1)], None, ALU.is_equal
                                      ).then_inc(carry_done, 1)

                def octets_to(ck):
                    return ck * OC + OC if not isinstance(ck, int) or ck < FULL else OCTETS

                def hots(q, par):
                    dve.tensor_tensor(onehot[:, par, :, :], cols[:, :].unsqueeze(1).to_broadcast([P, OT, P]),
                                      dst_rel[:, bass.ds(q * OT, OT)].unsqueeze(2).to_broadcast([P, OT, P]),
                                      ALU.is_equal).then_inc(hot_done, 1)

                def halve(q, par, t):
                    hold(dve, prod_done, PROD0 + 4 * (r * OCTETS + q) + t + 1)
                    dve.tensor_tensor(terms[:, par, t::4, NC + 1:], prod[:, t, :, 0:HW], prod[:, t, :, HW:MW],
                                      ALU.add).then_inc(half_done, 1)

                def octet(q, j, i, out_of=None):
                    par = j % 2
                    hold(dve, octet_summed, r * OCTETS + q + 1)
                    hots(q, par)
                    hold(dve, gathered[j], 128 * (r * NSLOT[j] + i + 1))
                    for t in range(4):
                        hold(dve, w_done, W0 + 4 * (r * OCTETS + q) + t + 1)
                        dve.tensor_tensor(
                            prod[:, t, :, :].rearrange("p b (i o) -> p b i o", i=NC),
                            bank[t][:, :].rearrange("p (b i o) -> p b i o", b=2, i=NC),
                            xg[:, j, t::4, :].unsqueeze(3).to_broadcast([P, 2, NC, NC]),
                            ALU.mult).then_inc(prod_done, 1)
                        if t == 1 and out_of is not None:
                            window_out(*out_of)
                            carry_hots(out_of[0] + 1, 1 - out_of[1])
                        if t >= 1:
                            halve(q, par, t - 1)
                    halve(q, par, 3)

                def turn(i, first=False):
                    for j in range(SIX):
                        out_of = None
                        if j == 1 and not first:
                            out_of = (i * 2 - 1, 1)
                        if j == OC + 1:
                            out_of = (i * 2, 0)
                        octet(i * SIX + j, j, i, out_of)

                def g_tile(t, last, i, j):
                    n = r * (TILES + 1) + t
                    step, own_at = n * STEPS0, n * 5 + r * 2
                    hold(dve, g_gathered[j], 16 * g_uses(r, i, j))
                    hold(dve, baton, step + 6)
                    g_after(dve.tensor_tensor(
                        g_prod[:, :].rearrange("p (i o) -> p i o", i=NC),
                        bank[0][:, 0:MW].rearrange("p (i o) -> p i o", i=NC),
                        g_x[:, :].unsqueeze(2).to_broadcast([P, NC, NC]), ALU.mult), own_at + 1)
                    dve.tensor_reduce(g_vals[:, NC + 1:], g_prod[:, :].rearrange("p (i o) -> p o i", i=NC), AX, ALU.add)
                    dve.tensor_copy(g_vals[:, 0:NC], g_x[:, :])
                    g_keys(step, own_at + 1, g_dst, last)
                    g_rows_of(step + 7, own_at + (3 if last else 1), GW)

                with dve.If(flag > 0):
                    turn(0, first=True)
                    with dve.Fori(1, PAIRS) as i:
                        turn(i)
                    octet(OCTETS - 1, 0, PAIRS)
                    window_out(FULL - 1, 1)
                    carry_hots(FULL, 0)
                    window_out(FULL, 0)
                with dve.Else():
                    tiles(dve, g_tile)

                hold(dve, agg_in, 16 * (r + 1))
                after(dve.tensor_scalar(inv[:, :], aggl[:, :, NC:NC + 1].rearrange("p j a -> p (j a)"), 1.0, None,
                                        ALU.max), 1)
                dve.reciprocal(inv[:, :], inv[:, :]).then_inc(own, 1)
                hold(dve, own, own_base(r) + 2)
                spread = inv[:, :].unsqueeze(2).to_broadcast([NP_, NJ, NC])
                dve.tensor_tensor(gin[:, :, 0:NC], aggl[:, :, 0:NC], spread, ALU.mult)
                dve.tensor_tensor(gin[:, :, NC:2 * NC], aggl[:, :, NC + 1:], spread, ALU.mult).then_inc(own, 1)

                def gate_out(u, par):
                    hold(dve, gate_summed, GU * r + u + 3)
                    dve.tensor_copy(gates[:, bass.ds(u * GT, GT), :],
                                    bank[2 + par][0:NP_, 0:GT * 4 * NC].rearrange("p (k f) -> p k f", k=GT)
                                    ).then_inc(gate_copied, 1)

                with dve.Fori(0, GU // 2) as v:
                    for par in range(2):
                        gate_out(v * 2 + par, par)
                gate_out(GU - 1, 0)
                hold(dve, act_gates, 2 * r + 1)
                g_r, g_z, g_n, g_h = (gates[:, :, NC * k:NC * (k + 1)] for k in range(4))
                h = gin[:, :, 2 * NC:3 * NC]
                after(dve.tensor_tensor(g_h, g_h, g_r, ALU.mult), 4)
                dve.tensor_tensor(g_n, g_n, g_h, ALU.add).then_inc(own, 1)
                hold(dve, act_gates, 2 * r + 2)
                after(dve.tensor_tensor(g_r, h, g_n, ALU.subtract), 6)
                after(dve.tensor_tensor(g_r, g_r, g_z, ALU.mult), 7)
                after(dve.tensor_tensor(h_new[:, :, :], g_n, g_r, ALU.add), 8)

            done = [own_base(REPEATS)]

            def link(ins):
                ins.then_inc(own, 1)
                done[0] += 1
                dve.wait_ge(own, done[0])

            def layernorm(n):
                mean, var, tmp = stat[:, 0, :], stat[:, 1, :], stat[:, 2, :]
                wide = lambda v: v.unsqueeze(2).to_broadcast([NP_, NJ, NC])
                link(dve.tensor_reduce(tmp, xs[:, :, :], AX, ALU.add))
                link(dve.tensor_scalar(mean, tmp, 1.0 / NC, None, ALU.mult))
                link(dve.tensor_tensor(xs[:, :, :], xs[:, :, :], wide(mean), ALU.subtract))
                link(dve.tensor_tensor(gates[:, :, 0:NC], xs[:, :, :], xs[:, :, :], ALU.mult))
                link(dve.tensor_reduce(tmp, gates[:, :, 0:NC], AX, ALU.add))
                link(dve.tensor_scalar(var, tmp, 1.0 / NC, EPS, ALU.mult, ALU.add))
                assert done[0] == OWN_LN[n]
                dve.wait_ge(ln_sqrt, n + 1)
                link(dve.reciprocal(tmp, var))
                return dve.tensor_tensor(xs[:, :, :], xs[:, :, :], wide(tmp), ALU.mult)

            link(dve.tensor_tensor(xs[:, :, :], xs[:, :, :], h_new[:, :, :], ALU.add))
            link(layernorm(0))
            assert done[0] == OWN_X2

            dve.wait_ge(table, 16 * (REPEATS + 1))

            def y_hots(q, par):
                hold(dve, y_turned, q + 1)
                dve.tensor_tensor(hot[:, par, :, :], cols[:, :].unsqueeze(1).to_broadcast([P, OT, P]),
                                  dst_rel[:, bass.ds(q * OT, OT)].unsqueeze(2).to_broadcast([P, OT, P]),
                                  ALU.is_equal).then_inc(y_hot, 1)

            def y_copy(q):
                par = q % 2
                if q + 2 < YOCTETS:
                    y_hots(q + 2, par)
                if q % OC == 0 and q // OC + 1 < YCHUNKS:
                    c = q // OC + 1
                    split(c, y_win[c % 2], 16 * (c // 2 + 1), c % 2)
                hold(dve, y_val, q + 3)
                hold(dve, y_stored[par], 16 * (q // 2 + 1))
                dve.tensor_copy(vals[:, par, :, :].rearrange("p k f -> p (k f)"), bank[4 + par][:, 0:P]
                                ).then_inc(y_copied, 1)

            def split_step(n, c, loaded, count, ch):
                if n == 0:
                    hold(dve, loaded, count)
                    hold(dve, split_done, c + 1)
                    dve.tensor_copy(ywin_parts[:, ch, 0, :], ywin[:, ch, :]).then_inc(own_split, 1)
                elif n == 1:
                    hold(dve, own_split, 3 * c + 1)
                    dve.tensor_tensor(rest[:, :], ywin[:, ch, :], ywin_parts[:, ch, 0, :], ALU.subtract
                                      ).then_inc(own_split, 1)
                elif n == 2:
                    hold(dve, own_split, 3 * c + 2)
                    dve.tensor_copy(ywin_parts[:, ch, 1, :], rest[:, :]).then_inc(own_split, 1)
                else:
                    hold(dve, own_split, 3 * c + 3)
                    dve.tensor_tensor(ywin_parts[:, ch, 2, :], rest[:, :], ywin_parts[:, ch, 1, :], ALU.subtract
                                      ).then_inc(split_done, 1)

            def split(*window):
                for n in range(4):
                    split_step(n, *window)

            def window1(j, i):
                ch = j // OC % 2
                return YCHUNKS + i * 2 + ch, ywin_in[ch], 16 * (i + 1), ch

            def hot_of_dst(q, j):
                par = j % 2
                hold(dve, turned1, 3 * q + 3)
                dve.tensor_tensor(hot[:, par, :, :], cols[:, :].unsqueeze(1).to_broadcast([P, OT, P]),
                                  dst_rel[:, bass.ds(q * OT, OT)].unsqueeze(2).to_broadcast([P, OT, P]),
                                  ALU.is_equal).then_inc(hot1, 1)

            def low_bits(q, j, i):
                par, ch, slot, d = j % 2, j // OC % 2, j % 3, DT[j % 2]
                g = j % OC * OT
                if j % OC == 0:
                    hold(dve, s1_in[ch], 16 * (i + 1))
                dve.tensor_scalar(src_low[:, par, :], src_i[:, ch, g:g + OT], P - 1, None, ALU.bitwise_and
                                  ).then_inc(own_hot, 1)
                if not (isinstance(q, int) and q == 0):
                    hold(dve, div_done, direct_before(q, j, i))
                hold(dve, placed_done, q + 1)
                dve.tensor_scalar(src_mod[:, slot, 0:d], src_i[:, ch, g + OT - d:g + OT], MODS - 1, None,
                                  ALU.bitwise_and).then_inc(own_hot, 1)

            def src_numbers(q, j):
                par, ch, slot, d = j % 2, j // OC % 2, j % 3, DT[j % 2]
                g = j % OC * OT
                hold(dve, own_hot, 4 * q + 2)
                dve.tensor_copy(src_lo[:, par, :], src_low[:, par, :]).then_inc(hot1, 1)
                dve.tensor_tensor(mod_hot[:, slot, 0:d, :], cols[:, 0:MODS].unsqueeze(1).to_broadcast([P, d, MODS]),
                                  src_mod[:, slot, 0:d].unsqueeze(2).to_broadcast([P, d, MODS]), ALU.is_equal
                                  ).then_inc(own_hot, 1)
                hold(dve, rows_done, q + 5)
                dve.tensor_copy(srcf[:, par, :], src_i[:, ch, g:g + OT]).then_inc(own_hot, 1)
                hold(dve, own_hot, 4 * q + 4)
                dve.tensor_tensor(src_hi[:, par, :], srcf[:, par, :], src_low[:, par, :], ALU.subtract
                                  ).then_inc(hot1, 1)
                dve.tensor_tensor(src_neg[:, slot, 0:d], src_mod[:, slot, 0:d], srcf[:, par, OT - d:], ALU.subtract
                                  ).then_inc(div_ready, 1)

            def octet1(q, j, i, ahead=True):
                par, slot, tiles = j % 2, j % 3, scattered_tiles(j % 2)
                q2, j2, i2 = q + 2, (j + 2) % SIX, i if j + 2 < SIX else i + 1
                splits = ahead and j2 % OC == 0
                hold(dve, m_done, q + 1)
                dve.tensor_scalar(away[:, 0:tiles], srcf[:, par, 0:tiles], -1.0, dummy[:, 0:1], ALU.mult, ALU.add
                                  ).then_inc(own1, 1)
                for h in range(2):
                    g, n = 4 * h, min(4, tiles - 4 * h)
                    hold(dve, turned1, EDGE0 + 3 * q + h + 1)
                    dve.tensor_tensor(
                        same[:, par, g:g + n, :], bank[6 + h][:, 0:n * P].rearrange("p (k e) -> p k e", k=n),
                        srcf[:, par, g:g + n].unsqueeze(2).to_broadcast([P, n, P]), ALU.is_equal
                    ).then_inc(same_done, 1)
                    if splits:
                        split_step(h, *window1(j2, i2))
                hold(dve, same_done, 2 * q + 6)
                dve.tensor_tensor(earlier[:, 0:tiles, :], same[:, par, 0:tiles, :],
                                  before_b[:, :].unsqueeze(1).to_broadcast([P, tiles, P]), ALU.mult).then_inc(own1, 1)
                if splits:
                    split_step(2, *window1(j2, i2))
                hold(dve, v_copied, q + 3)
                hold(dve, own_hot, 4 * q + 4)
                hold(dve, direct_done, direct_before(q, j, i) + 3 - DT[1 - par])
                for k, d, to in direct_tiles(par):
                    ins = dve.tensor_tensor(
                        placed[:, to, :, :].rearrange("p n (m f) -> p n m f", m=MODS),
                        val_parts[:, par, k, :, :].unsqueeze(2).to_broadcast([P, 3, MODS, NC]),
                        mod_hot[:, slot, d, :].unsqueeze(1).unsqueeze(3).to_broadcast([P, 3, MODS, NC]), ALU.mult)
                ins.then_inc(placed_done, 1)
                hold(dve, own1, 4 * q + 2)
                dve.tensor_reduce(count[:, 0:tiles], earlier[:, 0:tiles, :], AX, ALU.max).then_inc(own1, 1)
                if splits:
                    split_step(3, *window1(j2, i2))
                if ahead:
                    hot_of_dst(q2, j2)
                hold(dve, own1, 4 * q + 3)
                dve.tensor_tensor(shift[:, 0:tiles], count[:, 0:tiles], away[:, 0:tiles], ALU.mult).then_inc(own1, 1)
                if ahead:
                    low_bits(q2, j2, i2)
                hold(dve, own1, 4 * q + 4)
                hold(dve, scattered, q + 1)
                dve.tensor_tensor(rows[:, slot, 0:tiles], srcf[:, par, 0:tiles], shift[:, 0:tiles], ALU.add
                                  ).then_inc(rows_done, 1)
                if ahead:
                    src_numbers(q2, j2)

            def g_tile1(t, last, i, j):
                step, own_at = BATON1 + t * STEPS1, REPEATS * (5 * (TILES + 1) + 2) + 4 * t
                hold(dve, g_gathered[j], 16 * g_uses(REPEATS, i, j))
                dve.tensor_copy(g_vals[:, 0:NC], g_x[:, :])
                g_keys(step, own_at, g_src, last)
                g_rows_of(step + 2, own_at + (2 if last else 0), NC)

            with dve.If(flag > 0):
                for q in range(2):
                    y_hots(q, q)
                split(0, y_win[0], 16, 0)
                for q in range(YOCTETS):
                    y_copy(q)
                split(*window1(0, 0))
                for q in range(2):
                    hot_of_dst(q, q)
                    low_bits(q, q, 0)
                    src_numbers(q, q)
                with dve.Fori(0, PAIRS - 1) as i:
                    for j in range(SIX):
                        octet1(i * SIX + j, j, i)
                for q in range(OCTETS - SIX - 1, OCTETS):
                    octet1(q, q % SIX, q // SIX, ahead=(q + 2 < OCTETS))
                for b in range(SB):
                    parts_in = P if b < SB - 1 else BREST
                    dve.wait_ge(tot_turned, b + 1)
                    size = min(4 * P, (BLOCKS + 1 - 4 * b) * P)
                    dve.tensor_copy(tot_rows[0:parts_in, 4 * P * b:4 * P * b + size], bank[4 + b][0:parts_in, 0:size]
                                    ).then_inc(tot_out, 1)
            with dve.Else():
                tiles(dve, g_tile1)

            for k in range(ACCS):
                dve.wait_ge(acc_in[k], 16)
                link(dve.tensor_tensor(xs[:, :, :], xs[:, :, :],
                                       loaded_table(k).rearrange("p (j f) -> p j f", f=NC), ALU.add))
            layernorm(1).then_inc(result, 1)


PREP_SPAN, PREP_REL, PREP_FLAG = 6, 13, 17


def own_base(r):
    return r * 8


OWN_X2 = own_base(REPEATS) + 9
OWN_LN = [own_base(REPEATS) + 7, OWN_X2 + 8 + 6]
STEPS0, STEPS1 = 11, 6
BATON1 = REPEATS * (TILES + 1) * STEPS0

_INS = ['x', 'src', 'dst', 'edge_attr_13', 'L0_gnn_fnet_w1', 'L0_gnn_fnet_b1', 'L0_gnn_fnet_w2', 'L0_gnn_fnet_b2',
        'L0_gnn_gru_w_ih', 'L0_gnn_gru_w_hh', 'L0_gnn_gru_b_ih', 'L0_gnn_gru_b_hh']


def kernel(**inputs):
    import numpy as np
    import concourse.bacc as bacc
    from concourse import mybir
    from concourse.bass_utils import run_bass_kernel_spmd

    nc = bacc.Bacc("TRN2", target_bir_lowering=False, num_devices=1)
    arrays, args = {}, []
    for name in _INS:
        a = np.ascontiguousarray(inputs[name])
        arrays[f"in_{name}"] = a
        args.append(nc.dram_tensor(f"in_{name}", a.shape, mybir.dt.from_np(a.dtype), kind="ExternalInput").ap())
    args.append(nc.dram_tensor("out_0", (NODES, NC), mybir.dt.float32, kind="ExternalOutput").ap())
    program(nc, *args)
    run = run_bass_kernel_spmd(nc, [arrays], core_ids=[0])
    return run.results[0]["out_0"]
```
